# Optimizing a Trainium2 kernel written in Bass

```python
import numpy as np
import jax
import jax.numpy as jnp

def _softmax(x, axis=-1):
    return jax.nn.softmax(x, axis=axis)
def _gelu(x):
    return jax.nn.gelu(x, approximate=True)
def _silu(x):
    return jax.nn.silu(x)
def _sigmoid(x):
    return jax.nn.sigmoid(x)
def _layernorm(x, axis=-1, eps=1e-5):
    m = jnp.mean(x, axis=axis, keepdims=True)
    v = jnp.var(x, axis=axis, keepdims=True)
    return (x - m) / jnp.sqrt(v + eps)
def _scatter_add(tgt, idx, src, axis=0):
    return tgt.at[idx].add(src)
def _segment_sum(src, seg, n):
    return jax.ops.segment_sum(src, seg, n)

kernel_name = 'mk_adj_resnorm_d2_adj_256_9eb5e6'

def setup_inputs(seed: int = 0):
    np.random.seed(seed)
    _w = jnp.asarray
    def _rec_inputs():
        import jax
        import jax.numpy as jnp
        _gk = jax.random.key(seed)
        x = 7.22e-05 + 1 * jax.random.normal(jax.random.fold_in(_gk, 1), (16, 1024, 256), jnp.float32)
        _a = jax.random.bernoulli(jax.random.fold_in(_gk, 2), 0.0078125, (16, 1024, 1024))
        _a = jnp.logical_or(_a, jnp.swapaxes(_a, -1, -2))
        _a = jnp.logical_or(_a, jnp.eye(1024, dtype=bool))
        adj = _a.astype(jnp.int32)
        return x, adj
    x, adj = _rec_inputs()
    def _L0_gnn_setup():
        import jax, jax.numpy as jnp
        import numpy as np
        B, S, D = (64, 512, 256)

        def _leaky(x):
            return jnp.where(x >= 0, x, 0.2 * x)
        key = jax.random.key(seed)
        k = jax.random.split(key, 6)
        stdv = 1.0 / np.sqrt(D)
        return {'hidden': jax.random.normal(k[0], (B, S, D), dtype=jnp.float32), 'adj': jax.random.randint(k[1], (B, S, S), 0, 5, dtype=jnp.int32), 'a0': jax.random.uniform(k[2], (D, 1), jnp.float32, -stdv, stdv), 'a1': jax.random.uniform(k[3], (D, 1), jnp.float32, -stdv, stdv), 'a2': jax.random.uniform(k[4], (D, 1), jnp.float32, -stdv, stdv), 'a3': jax.random.uniform(k[5], (D, 1), jnp.float32, -stdv, stdv), 'bias': jnp.zeros((D,), dtype=jnp.float32)}
    _L0_gnn_all = _L0_gnn_setup()
    _L0_gnn_in = {k: v for k, v in _L0_gnn_all.items() if k in ('a0', 'a1', 'a2', 'a3', 'bias', )}
    del _L0_gnn_all

    def _L1_gnn_setup():
        import jax, jax.numpy as jnp
        import numpy as np
        NEG_INF = -1000000000.0
        LRELU_ALPHA = 0.2
        key = jax.random.key(seed)
        k1, k2, k3, k4, k5 = jax.random.split(key, 5)
        B, N, Din, H, F = (8, 1024, 256, 4, 64)
        X = jax.random.normal(k1, (B, N, Din), dtype=jnp.float32)
        A = jax.random.randint(k2, (B, N, N), 0, 2).astype(jnp.int32)
        W = jax.random.normal(k3, (Din, H * F), dtype=jnp.float32) * np.sqrt(2.0 / (Din + H * F))
        a_src = jax.random.normal(k4, (H, F), dtype=jnp.float32) * np.sqrt(2.0 / (1 + F))
        a_dst = jax.random.normal(k5, (H, F), dtype=jnp.float32) * np.sqrt(2.0 / (1 + F))
        return {'X': X, 'A': A, 'W': W, 'a_src': a_src, 'a_dst': a_dst}
    _L1_gnn_all = _L1_gnn_setup()
    _L1_gnn_in = {k: v for k, v in _L1_gnn_all.items() if k in ('W', 'a_src', 'a_dst', )}
    del _L1_gnn_all

    return {
        "x": x,
        "adj": adj,
        "L0_gnn_a0": _L0_gnn_in["a0"],
        "L0_gnn_a1": _L0_gnn_in["a1"],
        "L0_gnn_a2": _L0_gnn_in["a2"],
        "L0_gnn_a3": _L0_gnn_in["a3"],
        "L0_gnn_bias": _L0_gnn_in["bias"],
        "L1_gnn_W": _L1_gnn_in["W"],
        "L1_gnn_a_src": _L1_gnn_in["a_src"],
        "L1_gnn_a_dst": _L1_gnn_in["a_dst"],
    }

def reference(x, adj, L0_gnn_a0, L0_gnn_a1, L0_gnn_a2, L0_gnn_a3, L0_gnn_bias, L1_gnn_W, L1_gnn_a_src, L1_gnn_a_dst):
    import jax
    import jax.numpy as jnp
    def _L0_gnn_ref(hidden, adj, a0, a1, a2, a3, bias):
        import jax, jax.numpy as jnp
        import numpy as np
        B, S, D = (64, 512, 256)

        def _leaky(x):
            return jnp.where(x >= 0, x, 0.2 * x)
        h = hidden

        def e_of(a):
            return _leaky(jnp.einsum('bid,bjd->bij', h * a[:, 0], h))
        e0, e1, e2, e3 = (e_of(a0), e_of(a1), e_of(a2), e_of(a3))
        neg_inf = jnp.float32(-jnp.finfo(e0.dtype).max)
        alpha = jnp.where(adj == 1, e0, neg_inf)
        alpha = jnp.where(adj == 2, e1, alpha)
        alpha = jnp.where(adj == 3, e2, alpha)
        alpha = jnp.where(adj == 4, e3, alpha)
        alpha = jax.nn.sigmoid(alpha)
        return jnp.einsum('bij,bjd->bid', alpha, h) + bias

    def _L1_gnn_ref(X, A, W, a_src, a_dst):
        import jax, jax.numpy as jnp
        import numpy as np
        NEG_INF = -1000000000.0
        LRELU_ALPHA = 0.2
        B, N, _ = X.shape
        H, F = a_src.shape
        Wh = (X @ W).reshape(B, N, H, F)
        e_src = jnp.einsum('bnhf,hf->bnh', Wh, a_src)
        e_dst = jnp.einsum('bjhf,hf->bjh', Wh, a_dst)
        e = jax.nn.leaky_relu(e_src[:, :, None, :] + e_dst[:, None, :, :], LRELU_ALPHA)
        mask = (A > 0)[..., None]
        e = jnp.where(mask, e, NEG_INF)
        alpha = jax.nn.softmax(e, axis=2)
        Hout = jnp.einsum('bijh,bjhf->bihf', alpha, Wh)
        Hout = jax.nn.elu(Hout)
        return Hout.reshape(B, N, H * F)

    x = _layernorm(x + _L0_gnn_ref(x, adj, L0_gnn_a0, L0_gnn_a1, L0_gnn_a2, L0_gnn_a3, L0_gnn_bias), axis=-1)
    x = _layernorm(x + _L1_gnn_ref(x, adj, L1_gnn_W, L1_gnn_a_src, L1_gnn_a_dst), axis=-1)
    return x


_drawn_inputs = setup_inputs


def setup_inputs(seed=0):
    import zlib

    import numpy as np

    out = dict(_drawn_inputs(seed))
    spreads = {'L0_gnn_bias': (0.0, 0.1)}
    factors = {}
    for name, (base, spread) in spreads.items():
        noise = np.random.default_rng([zlib.crc32(name.encode()), seed]).standard_normal(out[name].shape)
        drawn = base * np.exp(spread * noise) if base else spread * noise
        out[name] = jnp.asarray(drawn.astype(out[name].dtype))
    for name, factor in factors.items():
        out[name] = (out[name] * factor).astype(out[name].dtype)
    return out
```

```python
from contextlib import ExitStack

import concourse.bass as bass
from concourse import mybir

P = 128
ALU = mybir.AluOpType
ACT = mybir.ActivationFunctionType
AX_X = mybir.AxisListType.X
F32 = mybir.dt.float32
I32 = mybir.dt.int32

LEAK = 0.2
LN_EPS = 1e-5
NEG_INF = -1e9


def general_path(nc, x, xT, adj, gates, bias, W, a_src, a_dst, out, flag=None):
    B, N, D = x.shape
    H, F = a_src.shape
    KT, RT, TYPES = D // P, N // P, gates.shape[2]
    HN = N // 2

    with ExitStack() as ctx:
        def sb(name, shape, dt=F32):
            return ctx.enter_context(nc.sbuf_tensor("g_" + name, shape, dt))

        def ps(name, shape, dt=F32):
            return ctx.enter_context(nc.psum_tensor("g_" + name, shape, dt))

        def sem(name):
            return ctx.enter_context(nc.semaphore("g_" + name))

        flag_sb = sb("flag_sb", [1, 1], I32)
        h_rows = sb("h_rows", [P, RT, D])
        h_cols = sb("h_cols", [P, KT, N])
        adj_rows = sb("adj_rows", [P, N], I32)
        gate_cols = sb("gate_cols", [P, KT, TYPES])
        bias_all = sb("bias_all", [P, D])
        W_sb = sb("W_sb", [P, KT, D])
        a_all = sb("a_all", [P, 2, D])
        wa_prod = sb("wa_prod", [P, D])
        wa = sb("wa", [P, KT, 2, H])
        wa_wide = sb("wa_wide", [P, KT, H, P])
        ones = sb("ones", [P, P])
        ident = sb("ident", [P, P])
        gated = sb("gated", [P, KT, P])
        picked = sb("picked", [P, N])
        scores = sb("scores", [P, N])
        in_range = sb("in_range", [P, N])
        weights = sb("weights", [P, N])
        masked = sb("masked", [P, N])
        weights_T = sb("weights_T", [P, RT, P])
        row = sb("row", [P, D])
        stats = sb("stats", [P, 6])
        moments = sb("moments", [P, 2])
        var = sb("var", [P, 1])
        std = sb("std", [P, 1])
        x1_rows = sb("x1_rows", [P, RT, D])
        x1_cols = sb("x1_cols", [P, KT, N])
        values = sb("values", [P, RT, D])
        src = sb("src", [P, RT, H])
        dst_all = sb("dst_all", [P, H, N])
        mask = sb("mask", [P, N])
        penalty = sb("penalty", [P, N])
        row_max = sb("row_max", [P, 1])
        row_sum = sb("row_sum", [P, 1])
        attended = sb("attended", [P, D])
        negative = sb("negative", [P, D])
        grown = sb("grown", [P, D])

        score_ps = ps("score_ps", [P, N])
        turn_ps = ps("turn_ps", [P, N])
        row_ps = ps("row_ps", [P, 512])
        wide_ps = ps("wide_ps", [P, 512])

        flag_in = sem("flag_in")
        constants_in = sem("constants_in")
        batch_in = sem("batch_in")
        adj_in = sem("adj_in")
        adj_used = sem("adj_used")
        stored = sem("stored")
        ident_zero = sem("ident_zero")
        ident_ready = sem("ident_ready")
        folded = sem("folded")
        gated_ready = sem("gated_ready")
        scores_ready = sem("scores_ready")
        leaked = sem("leaked")
        squashed = sem("squashed")
        masked_ready = sem("masked_ready")
        turned = sem("turned")
        turned_copied = sem("turned_copied")
        summed = sem("summed")
        var_ready = sem("var_ready")
        std_ready = sem("std_ready")
        x1_ready = sem("x1_ready")
        x1_turned = sem("x1_turned")
        x1_whole = sem("x1_whole")
        values_ready = sem("values_ready")
        values_copied = sem("values_copied")
        dst_ready = sem("dst_ready")
        dst_copied = sem("dst_copied")
        exp_in = sem("exp_in")
        exp_out = sem("exp_out")
        exp_turned = sem("exp_turned")
        exp_copied = sem("exp_copied")
        head_summed = sem("head_summed")
        negative_ready = sem("negative_ready")
        grown_ready = sem("grown_ready")
        out_ready = sem("out_ready")
        batch_done = sem("batch_done")

        def sync_program(sp):
            sp.dma_start(gate_cols[:], gates).then_inc(constants_in, 16)
            sp.dma_start(bias_all[:], bias.partition_broadcast(P)).then_inc(constants_in, 16)
            sp.dma_start(W_sb[:], W.rearrange("(c p) n -> p c n", p=P)).then_inc(constants_in, 16)
            for s, a in enumerate((a_src, a_dst)):
                sp.dma_start(a_all[:, s, :], a.rearrange("h f -> (h f)").partition_broadcast(P)).then_inc(constants_in, 16)
            with sp.Fori(0, B) as b:
                sp.wait_ge(batch_done, b + 1)
                sp.dma_start(h_rows[:], x[bass.ds(b, 1)].rearrange("a (t p) d -> p (a t) d", p=P)).then_inc(batch_in, 16)
                sp.dma_start(h_cols[:], xT[bass.ds(b, 1)].rearrange("a (c p) n -> p (a c) n", p=P)).then_inc(batch_in, 16)
                with sp.Fori(0, RT) as t:
                    sp.wait_ge(adj_used, b * (2 * RT) + t + 1)
                    sp.dma_start(adj_rows[:], adj[bass.ds(b, 1), bass.ds(t * P, P)].rearrange("a p n -> p (a n)")
                                 ).then_inc(adj_in, 16)
                with sp.Fori(0, RT) as t:
                    sp.wait_ge(adj_used, b * (2 * RT) + t + RT + 1)
                    sp.dma_start(adj_rows[:], adj[bass.ds(b, 1), bass.ds(t * P, P)].rearrange("a p n -> p (a n)")
                                 ).then_inc(adj_in, 16)
                    sp.wait_ge(out_ready, b * RT + t + 1)
                    sp.dma_start(out[bass.ds(b, 1), bass.ds(t * P, P)].rearrange("a p n -> p (a n)"), row[:]
                                 ).then_inc(stored, 16)
            sp.wait_ge(stored, B * RT * 16)

        def gpsimd_program(pool):
            nc.gpsimd.memset(ident[:], 0.0).then_inc(ident_zero, 1)
            pool.wait_ge(ident_zero, 1)
            nc.gpsimd.affine_select(out=ident[:], in_=ident[:], compare_op=ALU.not_equal, fill=1.0,
                                    base=0, pattern=[[-1, P]], channel_multiplier=1).then_inc(ident_ready, 1)

        def scalar_program(act):
            with act.Fori(0, B) as b:
                with act.Fori(0, RT) as t:
                    act.wait_ge(leaked, b * RT + t + 1)
                    nc.scalar.activation(weights[:], scores[:], ACT.Sigmoid).then_inc(squashed, 1)
                    act.wait_ge(var_ready, b * (2 * RT) + t + 1)
                    nc.scalar.activation(std[:], var[:], ACT.Sqrt).then_inc(std_ready, 1)
                with act.Fori(0, RT) as t:
                    for h in range(H):
                        act.wait_ge(exp_in, (b * RT + t) * H + h + 1)
                        nc.scalar.activation(weights[:], scores[:], ACT.Exp, accum_out=row_sum[:]).then_inc(exp_out, 1)
                    act.wait_ge(negative_ready, b * RT + t + 1)
                    nc.scalar.activation(grown[:], negative[:], ACT.Exp).then_inc(grown_ready, 1)
                    act.wait_ge(var_ready, b * (2 * RT) + t + RT + 1)
                    nc.scalar.activation(std[:], var[:], ACT.Sqrt).then_inc(std_ready, 1)

        def tensor_program(pe):
            pe.wait_ge(ident_ready, 1)
            pe.wait_ge(folded, 1)
            with pe.Fori(0, B) as b:
                with pe.Fori(0, RT) as t:
                    n = b * RT + t
                    pe.wait_ge(batch_in, b * 32 + 32)
                    for k in range(TYPES):
                        pe.wait_ge(gated_ready, n * TYPES + k + 1)
                        for half in range(2):
                            cut = slice(half * HN, (half + 1) * HN)
                            for c in range(KT):
                                last = nc.tensor.matmul(score_ps[:, cut], gated[:, c, :], h_cols[:, c, cut],
                                                        start=(c == 0), stop=(c == KT - 1))
                        last.then_inc(scores_ready, 1)
                    pe.wait_ge(masked_ready, n + 1)
                    for j in range(RT):
                        last = nc.tensor.transpose(turn_ps[:, j * P:(j + 1) * P], masked[:, j * P:(j + 1) * P], ident[:])
                    last.then_inc(turned, 1)
                    pe.wait_ge(turned_copied, n + 1)
                    for j in range(RT):
                        last = nc.tensor.matmul(row_ps[:, 0:D], weights_T[:, j, :], h_rows[:, j, :],
                                                start=(j == 0), stop=(j == RT - 1))
                    last.then_inc(summed, 1)
                    pe.wait_ge(x1_ready, n + 1)
                    for c in range(KT):
                        last = nc.tensor.transpose(wide_ps[:, c * P:(c + 1) * P], row[:, c * P:(c + 1) * P], ident[:])
                    last.then_inc(x1_turned, 1)
                pe.wait_ge(x1_whole, b + 1)
                for t in range(RT):
                    if t >= 1:
                        pe.wait_ge(values_copied, b * RT + t)
                    for c in range(KT):
                        nc.tensor.matmul(row_ps[:, 0:D], x1_cols[:, c, t * P:(t + 1) * P], W_sb[:, c, :],
                                         start=(c == 0), stop=(c == KT - 1))
                    for c in range(KT):
                        last = nc.tensor.matmul(wide_ps[:, 0:H], x1_cols[:, c, t * P:(t + 1) * P], wa[:, c, 0, :],
                                                start=(c == 0), stop=(c == KT - 1))
                    last.then_inc(values_ready, 1)
                pe.wait_ge(values_copied, b * RT + RT)
                for n in range(2 * H):
                    cut = slice(n % 2 * HN, (n % 2 + 1) * HN)
                    if n >= 1:
                        pe.wait_ge(dst_copied, b * (2 * H) + n)
                    for c in range(KT):
                        last = nc.tensor.matmul(wide_ps[:, 0:HN], wa_wide[:, c, n // 2, :], x1_cols[:, c, cut],
                                                start=(c == 0), stop=(c == KT - 1))
                    last.then_inc(dst_ready, 1)
                with pe.Fori(0, RT) as t:
                    n = b * RT + t
                    for h in range(H):
                        pe.wait_ge(exp_out, n * H + h + 1)
                        for j in range(RT):
                            last = nc.tensor.transpose(turn_ps[:, j * P:(j + 1) * P], weights[:, j * P:(j + 1) * P], ident[:])
                        last.then_inc(exp_turned, 1)
                        pe.wait_ge(exp_copied, n * H + h + 1)
                        for j in range(RT):
                            last = nc.tensor.matmul(row_ps[:, 0:F], weights_T[:, j, :], values[:, j, h * F:(h + 1) * F],
                                                    start=(j == 0), stop=(j == RT - 1))
                        last.then_inc(head_summed, 1)

        def vector_program(dve):
            def std_of_row(nth):
                nc.vector.bn_stats(stats[:], row[:])
                dve.drain()
                nc.vector.bn_aggr(moments[:], stats[:])
                dve.drain()
                nc.vector.tensor_scalar_add(var[:], moments[:, 1:2], LN_EPS).then_inc(var_ready, 1)
                dve.wait_ge(std_ready, nth)
                nc.vector.reciprocal(var[:], std[:])
                dve.drain()

            nc.vector.memset(stats[:], 0.0).then_inc(batch_done, 1)
            nc.vector.memset(row_max[:], 0.0).then_inc(adj_used, 1)
            dve.wait_ge(constants_in, 80)
            nc.vector.memset(ones[:], 1.0)
            for c in range(KT):
                for s in range(2):
                    dve.drain()
                    nc.vector.tensor_tensor(wa_prod[:], W_sb[:, c, :], a_all[:, s, :], ALU.mult)
                    dve.drain()
                    nc.vector.reduce_sum(wa[:, c, s, :], wa_prod[:].rearrange("p (h f) -> p h f", h=H), AX_X)
            dve.drain()
            for c in range(KT):
                for h in range(H):
                    last = nc.vector.tensor_scalar(wa_wide[:, c, h, :], ones[:], wa[:, c, 1, h:h + 1], None, ALU.mult)
            last.then_inc(folded, 1)
            dve.drain()

            with dve.Fori(0, B) as b:
                with dve.Fori(0, RT) as t:
                    n = b * RT + t
                    dve.wait_ge(batch_in, b * 32 + 32)
                    dve.wait_ge(adj_in, (b * (2 * RT) + t) * 16 + 16)
                    for k in range(TYPES):
                        for c in range(KT):
                            last = nc.vector.tensor_scalar(gated[:, c, :], h_cols[:, c, bass.ds(t * P, P)],
                                                           gate_cols[:, c, k:k + 1], None, ALU.mult)
                        last.then_inc(gated_ready, 1)
                        dve.wait_ge(scores_ready, n * TYPES + k + 1)
                        dst = scores if k else picked
                        nc.vector.scalar_tensor_tensor(dst[:], adj_rows[:], float(k + 1), score_ps[:],
                                                       ALU.is_equal, ALU.mult)
                        dve.drain()
                        if k:
                            nc.vector.tensor_tensor(picked[:], picked[:], scores[:], ALU.add)
                            dve.drain()
                    nc.vector.scalar_tensor_tensor(scores[:], picked[:], LEAK, picked[:], ALU.mult, ALU.max).then_inc(leaked, 1)
                    nc.vector.tensor_scalar(in_range[:], adj_rows[:], 1.0, None, ALU.is_ge)
                    dve.drain()
                    nc.vector.scalar_tensor_tensor(penalty[:], adj_rows[:], float(TYPES), in_range[:],
                                                   ALU.is_le, ALU.mult).then_inc(adj_used, 1)
                    dve.drain()
                    dve.wait_ge(squashed, n + 1)
                    nc.vector.tensor_tensor(masked[:], weights[:], penalty[:], ALU.mult).then_inc(masked_ready, 1)
                    dve.wait_ge(turned, n + 1)
                    nc.vector.tensor_copy(weights_T[:].rearrange("p t q -> p (t q)"), turn_ps[:]).then_inc(turned_copied, 1)
                    dve.wait_ge(summed, n + 1)
                    nc.vector.tensor_tensor(row[:], row_ps[:, 0:D], bias_all[:], ALU.add)
                    dve.drain()
                    nc.vector.tensor_tensor(row[:], row[:], h_rows[:, bass.ds(t, 1), :].rearrange("p a d -> p (a d)"), ALU.add)
                    dve.drain()
                    std_of_row(b * (2 * RT) + t + 1)
                    nc.vector.tensor_scalar(row[:], row[:], moments[:, 0:1], var[:], ALU.subtract, ALU.mult).then_inc(x1_ready, 1)
                    dve.drain()
                    nc.vector.tensor_copy(x1_rows[:, bass.ds(t, 1), :].rearrange("p a d -> p (a d)"), row[:])
                    dve.wait_ge(x1_turned, n + 1)
                    nc.vector.tensor_copy(x1_cols[:, :, bass.ds(t * P, P)], wide_ps[:, 0:D].rearrange("p (c q) -> p c q", c=KT))
                    dve.drain()
                nc.vector.memset(stats[:], 0.0).then_inc(x1_whole, 1)
                for t in range(RT):
                    dve.wait_ge(values_ready, b * RT + t + 1)
                    nc.vector.tensor_copy(src[:, t, :], wide_ps[:, 0:H])
                    dve.drain()
                    nc.vector.tensor_copy(values[:, t, :], row_ps[:, 0:D]).then_inc(values_copied, 1)
                for m in range(2 * H):
                    dve.wait_ge(dst_ready, b * (2 * H) + m + 1)
                    nc.vector.tensor_copy(dst_all[:, m // 2, m % 2 * HN:(m % 2 + 1) * HN], wide_ps[:, 0:HN]).then_inc(dst_copied, 1)
                dve.drain()
                with dve.Fori(0, RT) as t:
                    n = b * RT + t
                    dve.wait_ge(adj_in, (b * (2 * RT) + t) * 16 + RT * 16 + 16)
                    nc.vector.tensor_scalar(mask[:], adj_rows[:], 0.0, None, ALU.is_gt).then_inc(adj_used, 1)
                    dve.drain()
                    nc.vector.tensor_scalar(penalty[:], mask[:], -NEG_INF, NEG_INF, ALU.mult, ALU.add)
                    dve.drain()
                    for h in range(H):
                        nc.vector.tensor_scalar(picked[:], dst_all[:, h, :], src[:, bass.ds(t, 1), h:h + 1].rearrange("p a h -> p (a h)"),
                                                None, ALU.add)
                        dve.drain()
                        nc.vector.scalar_tensor_tensor(scores[:], picked[:], LEAK, picked[:], ALU.mult, ALU.max)
                        dve.drain()
                        nc.vector.tensor_tensor(picked[:], scores[:], mask[:], ALU.mult)
                        dve.drain()
                        nc.vector.tensor_tensor(scores[:], picked[:], penalty[:], ALU.add)
                        dve.drain()
                        nc.vector.reduce_max(row_max[:], scores[:], AX_X)
                        dve.drain()
                        nc.vector.tensor_scalar(scores[:], scores[:], row_max[:], None, ALU.subtract).then_inc(exp_in, 1)
                        dve.wait_ge(exp_turned, n * H + h + 1)
                        nc.vector.tensor_copy(weights_T[:].rearrange("p t q -> p (t q)"), turn_ps[:]).then_inc(exp_copied, 1)
                        nc.vector.reciprocal(row_max[:], row_sum[:])
                        dve.drain()
                        dve.wait_ge(head_summed, n * H + h + 1)
                        nc.vector.tensor_scalar(attended[:, h * F:(h + 1) * F], row_ps[:, 0:F], row_max[:], None, ALU.mult)
                        dve.drain()
                    nc.vector.tensor_scalar(negative[:], attended[:], 0.0, None, ALU.min).then_inc(negative_ready, 1)
                    dve.wait_ge(grown_ready, n + 1)
                    nc.vector.tensor_scalar(grown[:], grown[:], 1.0, None, ALU.subtract)
                    dve.drain()
                    nc.vector.scalar_tensor_tensor(attended[:], attended[:], 0.0, grown[:], ALU.max, ALU.add)
                    dve.drain()
                    nc.vector.tensor_tensor(row[:], attended[:], x1_rows[:, bass.ds(t, 1), :].rearrange("p a d -> p (a d)"), ALU.add)
                    dve.drain()
                    std_of_row(b * (2 * RT) + t + RT + 1)
                    nc.vector.tensor_scalar(row[:], row[:], moments[:, 0:1], var[:], ALU.subtract, ALU.mult).then_inc(out_ready, 1)
                    dve.drain()
                    dve.wait_ge(stored, n * 16 + 16)
                nc.vector.memset(stats[:], 0.0).then_inc(batch_done, 1)
                dve.drain()

        block = ctx.enter_context(nc.Block())

        def when_flagged(eng, program):
            if flag is None:
                program(eng)
                return
            raw = eng.value_load(flag_sb[0:1, 0:1])
            with eng.If(raw > 0):
                program(eng)

        @block.sync
        def _(sp):
            when_flagged(sp, sync_program)

        @block.gpsimd
        def _(pool):
            when_flagged(pool, gpsimd_program)

        @block.scalar
        def _(act):
            when_flagged(act, scalar_program)

        @block.tensor
        def _(pe):
            when_flagged(pe, tensor_program)

        @block.vector
        def _(dve):
            when_flagged(dve, vector_program)


def kernel(x, adj, L0_gnn_a0, L0_gnn_a1, L0_gnn_a2, L0_gnn_a3, L0_gnn_bias, L1_gnn_W, L1_gnn_a_src, L1_gnn_a_dst):
    import numpy as np
    import concourse.bacc as bacc
    from concourse.bass_utils import run_bass_kernel_spmd

    x, adj = np.asarray(x), np.asarray(adj)
    arrays = {
        "x": x,
        "xT": np.ascontiguousarray(x.transpose(0, 2, 1)),
        "adj": adj,
        "gates": np.ascontiguousarray(np.stack([np.asarray(a).reshape(-1, P).T for a in
                                                (L0_gnn_a0, L0_gnn_a1, L0_gnn_a2, L0_gnn_a3)], axis=2)),
        "bias": np.asarray(L0_gnn_bias),
        "W": np.asarray(L1_gnn_W),
        "a_src": np.asarray(L1_gnn_a_src),
        "a_dst": np.asarray(L1_gnn_a_dst),
    }
    nc = bacc.Bacc("TRN2", target_bir_lowering=False, num_devices=1)
    args = {n: nc.dram_tensor("in_" + n, a.shape, mybir.dt.from_np(a.dtype), kind="ExternalInput").ap()
            for n, a in arrays.items()}
    out = nc.dram_tensor("out", x.shape, F32, kind="ExternalOutput").ap()
    general_path(nc, **args, out=out)
    r = run_bass_kernel_spmd(nc, [{"in_" + n: a for n, a in arrays.items()}], core_ids=[0])
    return r.results[0]["out"]
```

```python
import math
from contextlib import ExitStack

import concourse.bass as bass
from concourse import mybir

P = 128
ALU = mybir.AluOpType
ACT = mybir.ActivationFunctionType
AX_X = mybir.AxisListType.X
AX_XY = mybir.AxisListType.XY
F16 = mybir.dt.float16
F32 = mybir.dt.float32
I32 = mybir.dt.int32

LEAK = 0.2
LN_EPS = 1e-5
NEG_INF = -1e9


def fast_path(nc, x, xT, adjT, gates, bias, W, a_src, a_dst, out, flag_sb):
    B, N, D = x.shape
    H, F = a_src.shape
    KT, RT = D // P, N // P
    HN = N // 2
    F1 = F + 1
    DX = D + 2 * H
    BANK = 512
    SLOTS = 4
    SCALE = 64.0
    LOG_VALUE_SCALE = math.log(512.0)
    CHECK_AT = [RT, RT + 1, RT + 1 + H, RT + 1 + 2 * H]
    CHECK_AT += [CHECK_AT[-1] + n for n in (1, 2, 3, 4)]
    CHECKS = CHECK_AT[-1]
    SQUARES_MOST, RANGE_MOST, SHIFT_MOST = 2.0 ** 18, 14.0, 60.0
    TINY = 1e-6
    W_SQ_MOST, W_NORM_MOST, GATE_SQ_MOST = 900.0 ** 2, 60.0, 1.9 ** 2

    with ExitStack() as ctx:
        def sb(name, shape, dt=F32):
            return ctx.enter_context(nc.sbuf_tensor(name, shape, dt))

        def sem(name):
            return ctx.enter_context(nc.semaphore(name))

        x_rows = sb("x_rows", [P, RT, D])
        x_cols = sb("x_cols", [P, KT, N])
        adj_cols = sb("adj_cols", [P, SLOTS, N], I32)
        edge = sb("edge", [P, RT, N], F16)
        gate_in = sb("gate_in", [P, KT, 4])
        gate = sb("gate", [P, KT])
        bias_all = sb("bias_all", [P, D])
        W_ext = sb("W_ext", [P, KT, DX])
        W_hi = sb("W_hi", [P, KT, DX], F16)
        W_lo = sb("W_lo", [P, KT, DX], F16)
        ones = sb("ones", [P, P])
        ident = sb("ident", [P, P])
        minus_half = sb("minus_half", [P, RT])
        log_scale = sb("log_scale", [P, 1])
        minus_one = sb("minus_one", [P, 1])
        head_pick = sb("head_pick", [64, H, P], F16)
        cols_hi = sb("cols_hi", [P, KT, N], F16)
        cols_lo = sb("cols_lo", [P, KT, N], F16)
        gated_hi = sb("gated_hi", [P, KT, N], F16)
        gated_lo = sb("gated_lo", [P, KT, N], F16)
        x_bias = sb("x_bias", [P, RT, D])
        slopes = sb("slopes", [P, 4, N])
        alpha = sb("alpha", [P, 2, N])
        weights = sb("weights", [P, RT, N])
        stats = sb("stats", [P, RT, 6])
        moments = sb("moments", [P, RT, 2])
        var = sb("var", [P, RT])
        rstd = sb("rstd", [P, RT])
        x1_rows = sb("x1_rows", [P, RT, D])
        x1_hi = sb("x1_hi", [P, RT, KT, P], F16)
        x1_lo = sb("x1_lo", [P, RT, KT, P], F16)
        values = sb("values", [P, RT, H, F1])
        sd = sb("sd", [P, RT, 2, H])
        peaks = sb("peaks", [P, 3, H])
        own_peaks = sb("own_peaks", [P, 3, H])
        tops = sb("tops", [P, 3, H])
        dst_neg = sb("dst_neg", [P, RT, H])
        dst_rel = sb("dst_rel", [P, RT, H])
        src_rel = sb("src_rel", [P, RT, H])
        exp_full = sb("exp_full", [P, RT, H])
        exp_leak = sb("exp_leak", [P, RT, H])
        exp_src = sb("exp_src", [P, RT, H])
        prod_full = sb("prod_full", [P, RT, H, F1])
        prod_leak = sb("prod_leak", [P, RT, H, F1])
        step_rhs = sb("step_rhs", [P, 2, RT, H, 2 * F1], F16)
        edge_rhs = sb("edge_rhs", [P, 2, RT, H, F1], F16)
        src_rows = sb("src_rows", [64, N], F16)
        boosted = sb("boosted", [P, RT, F1])
        inv_sum = sb("inv_sum", [P, RT, H])
        least = sb("least", [P, 1])
        gate_sq = sb("gate_sq", [P, KT])
        seen = sb("seen", [P, CHECKS])
        worst = sb("worst", [P, CHECKS])
        limit = sb("limit", [P, CHECKS])
        beyond = sb("beyond", [P, 1])
        beyond_any = sb("beyond_any", [P, 1])

        gated = alpha
        src_all = slopes
        step = weights[:].bitcast(F16).rearrange("p t (u n) -> p (t u) n", u=2).rearrange("p (g t) n -> p g t n", g=2)
        flat = weights[:].rearrange("p t n -> p (t n)")
        W_sq = flat[:, 0:KT * DX].rearrange("p (c n) -> p c n", c=KT)
        a_all = flat[:, N:N + 2 * D].rearrange("p (s n) -> p s n", s=2)
        wa_prod = flat[:, 2 * N:2 * N + KT * 2 * D].rearrange("p (c s n) -> p c s n", c=KT, s=2)
        unused = x1_lo[:].rearrange("p t c q -> p (t c q)")[:, 0:N]
        attended = prod_full
        heads = attended[:].rearrange("p t h f -> p (t h) f")
        grown = values[:].rearrange("p t h f -> p (t h f)")[:, 0:RT * D].rearrange("p (m f) -> p m f", f=F)
        out_rows = prod_leak[:].rearrange("p t h f -> p (t h f)")[:, 0:RT * D].rearrange("p (t d) -> p t d", d=D)

        ps = ctx.enter_context(nc.psum_tensor("ps", [P, 8, BANK], F32))

        def banks(first, count):
            return ps[:, first:first + count, :].rearrange("p b n -> p (b n)")

        SRC_BANKS = (2, 4, 6, 2)
        GROUPS = [(g * 3, min(3, RT - g * 3)) for g in range((RT + 2) // 3)]
        NG = len(GROUPS)

        constants_in = sem("constants_in")
        x_cols_in = sem("x_cols_in")
        x_rows_in = sem("x_rows_in")
        adj_in = [sem(f"adj_in{n}") for n in range(SLOTS)]
        stored = sem("stored")
        out_free = sem("out_free")
        consts_made = sem("consts_made")
        pool_consts = sem("pool_consts")
        w_whole = sem("w_whole")
        w_split = sem("w_split")
        norms_ready = sem("norms_ready")
        cols_high = sem("cols_high")
        cols_split = sem("cols_split")
        gated_ready = sem("gated_ready")
        gated_high = sem("gated_high")
        gated_split = sem("gated_split")
        biased = sem("biased")
        edge_built = sem("edge_built")
        adj_checked = sem("adj_checked")
        scored = sem("scored")
        squashed = sem("squashed")
        alpha_ready = sem("alpha_ready")
        turned = sem("turned")
        masked = sem("masked")
        summed = sem("summed")
        sum_taken = sem("sum_taken")
        var_ready = sem("var_ready")
        rstd_ready = sem("rstd_ready")
        x1_ready = sem("x1_ready")
        x1_turned = sem("x1_turned")
        x1_high = sem("x1_high")
        x1_split = sem("x1_split")
        ones_set = sem("ones_set")
        values_ready = sem("values_ready")
        values_taken = sem("values_taken")
        rows_ready = sem("rows_ready")
        rows_high = sem("rows_high")
        rows_split = sem("rows_split")
        src_spread = sem("src_spread")
        src_copied = sem("src_copied")
        peaks_ready = sem("peaks_ready")
        tops_ready = sem("tops_ready")
        relative = sem("relative")
        exps_ready = sem("exps_ready")
        full_ready = sem("full_ready")
        leak_ready = sem("leak_ready")
        full_high = sem("full_high")
        leak_high = sem("leak_high")
        rhs_ready = sem("rhs_ready")
        step_ready = sem("step_ready")
        bank_done = sem("bank_done")
        bank_taken = sem("bank_taken")
        negative_ready = sem("negative_ready")
        grown_ready = sem("grown_ready")
        var1_ready = sem("var1_ready")
        rstd1_ready = sem("rstd1_ready")
        out_ready = sem("out_ready")
        beyond_ready = sem("beyond_ready")
        beyond_reduced = sem("beyond_reduced")

        def over_batches(eng, prepare, main):
            prepare(0)
            with eng.Fori(0, B - 1) as b:
                main(b, lambda: prepare(b + 1))
            main(B - 1, lambda: None)

        block = ctx.enter_context(nc.Block())

        @block.sync
        def _(sp):
            sp.dma_start(gate_in[:], gates).then_inc(constants_in, 16)
            sp.dma_start(bias_all[:], bias.partition_broadcast(P)).then_inc(constants_in, 16)
            sp.dma_start(W_ext[:, :, 0:D], W.rearrange("(c p) n -> p c n", p=P)).then_inc(constants_in, 16)
            for s, a in enumerate((a_src, a_dst)):
                sp.dma_start(a_all[:, s, :], a.rearrange("h f -> (h f)").partition_broadcast(P)).then_inc(constants_in, 16)

            def load_adj(b, t):
                sp.dma_start(adj_cols[:, t % SLOTS, :], adjT[bass.ds(b, 1), t * P:(t + 1) * P].rearrange("a p n -> p (a n)")
                             ).then_inc(adj_in[t % SLOTS], 16)

            def load_x(b):
                sp.dma_start(x_cols[:], xT[bass.ds(b, 1)].rearrange("a (c p) n -> p (a c) n", p=P)).then_inc(x_cols_in, 16)

            def load_rows(b):
                sp.dma_start(x_rows[:], x[bass.ds(b, 1)].rearrange("a (t p) d -> p (a t) d", p=P)).then_inc(x_rows_in, 16)

            def late_adj(b):
                for t in range(SLOTS, RT):
                    sp.wait_ge(edge_built, b * RT + t - SLOTS + 1)
                    sp.wait_ge(adj_checked, b * RT + t - SLOTS + 1)
                    load_adj(b, t)

            def prepare(b):
                if isinstance(b, int) and b == 0:
                    load_x(b)
                    load_rows(b)
                    for t in range(SLOTS):
                        load_adj(b, t)
                    return
                sp.wait_ge(cols_split, b)
                sp.wait_ge(gated_ready, b)
                load_x(b)
                for t in range(SLOTS):
                    sp.wait_ge(edge_built, b * RT + t - SLOTS + 1)
                    sp.wait_ge(adj_checked, b * RT + t - SLOTS + 1)
                    load_adj(b, t)
                sp.wait_ge(summed, b * RT)
                load_rows(b)

            def main(b, prepare_next):
                late_adj(b)
                prepare_next()
                for half in range(2):
                    cut = slice(half * RT // 2, (half + 1) * RT // 2)
                    sp.wait_ge(out_ready, b * 2 + half + 1)
                    sp.dma_start(out[bass.ds(b, 1)].rearrange("a (t p) d -> p (a t) d", p=P)[:, cut, :], out_rows[:, cut, :]
                                 ).then_inc(stored, 16)
                sp.wait_ge(stored, b * 32 + 32)
                sp.sem_inc(out_free, 1)

            sp.sem_inc(out_free, 1)
            over_batches(sp, prepare, main)
            sp.wait_ge(stored, B * 32)

        @block.gpsimd
        def _(pool):
            nc.gpsimd.memset(ident[:], 0.0)
            nc.gpsimd.memset(head_pick[:], 0.0)
            pool.drain()
            nc.gpsimd.affine_select(out=ident[:], in_=ident[:], compare_op=ALU.not_equal, fill=1.0,
                                    base=0, pattern=[[-1, P]], channel_multiplier=1)
            for part in range(2):
                pool.drain()
                block_of = head_pick[32 * part:32 * part + 32]
                nc.gpsimd.affine_select(out=block_of, in_=block_of, compare_op=ALU.not_equal, fill=1.0,
                                        base=0, pattern=[[-1, H], [0, P]], channel_multiplier=1)
            pool.drain()
            nc.gpsimd.memset(src_rows[:], 0.0).then_inc(pool_consts, 1)
            pool.wait_ge(constants_in, 80)
            pool.wait_ge(consts_made, 1)

            def prepare(b):
                pool.wait_ge(cols_high, b + 1)
                nc.gpsimd.tensor_tensor(cols_lo[:], x_cols[:], cols_hi[:], ALU.subtract).then_inc(cols_split, 1)
                pool.wait_ge(gated_high, b + 1)
                nc.gpsimd.tensor_tensor(gated_lo[:], gated[:], gated_hi[:], ALU.subtract).then_inc(gated_split, 1)
                pool.wait_ge(x_rows_in, b * 16 + 16)
                nc.gpsimd.tensor_tensor(x_bias[:], x_rows[:], bias_all[:].rearrange("p (a d) -> p a d", a=1).to_broadcast([P, RT, D]),
                                        ALU.add).then_inc(biased, 1)

            def main(b, prepare_next):
                for t in range(RT):
                    pool.wait_ge(var_ready, b * RT + t + 1)
                    nc.gpsimd.tensor_tensor(rstd[:, t:t + 1], var[:, t:t + 1], minus_half[:, t:t + 1], ALU.pow).then_inc(rstd_ready, 1)
                pool.wait_ge(peaks_ready, b + 1)
                nc.gpsimd.tensor_tensor(own_peaks[:], peaks[:], ones[:, 0:3 * H].rearrange("p (k h) -> p k h", k=3), ALU.mult)
                pool.drain()
                nc.gpsimd.partition_all_reduce(tops[:].rearrange("p k h -> p (k h)"), own_peaks[:].rearrange("p k h -> p (k h)"),
                                               P, bass.bass_isa.ReduceOp.max).then_inc(tops_ready, 1)
                pool.wait_ge(exps_ready, b + 1)
                pool.wait_ge(out_free, b + 1)
                nc.gpsimd.tensor_tensor(prod_leak[:], values[:], exp_leak[:].rearrange("p t (h o) -> p t h o", o=1).to_broadcast([P, RT, H, F1]),
                                        ALU.mult).then_inc(leak_ready, 1)
                prepare_next()
                for half in range(2):
                    cut = slice(half * RT // 2, (half + 1) * RT // 2)
                    pool.wait_ge(var1_ready, b * 2 + half + 1)
                    nc.gpsimd.tensor_tensor(rstd[:, cut], var[:, cut], minus_half[:, cut], ALU.pow).then_inc(rstd1_ready, 1)

            over_batches(pool, prepare, main)
            pool.wait_ge(beyond_ready, 1)
            nc.gpsimd.partition_all_reduce(beyond_any[:], beyond[:], P, bass.bass_isa.ReduceOp.max).then_inc(beyond_reduced, 1)

        @block.scalar
        def _(act):
            def check_adj(b, t):
                act.wait_ge(adj_in[t % SLOTS], b * (RT // SLOTS * 16) + t // SLOTS * 16 + 16)
                nc.scalar.activation(unused, adj_cols[:, t % SLOTS, :], ACT.Relu, bias=minus_one[:],
                                     accum_out=seen[:, t:t + 1]).then_inc(adj_checked, 1)
                act.drain()

            def prepare(b):
                act.wait_ge(x_cols_in, b * 16 + 16)
                act.wait_ge(consts_made, 1)
                nc.scalar.activation(cols_hi[:], x_cols[:], ACT.Copy).then_inc(cols_high, 1)
                nc.scalar.activation(gated_hi[:], x_cols[:], ACT.Square, accum_out=seen[:, RT:RT + 1])
                act.drain()
                act.wait_ge(gated_ready, b + 1)
                nc.scalar.activation(gated_hi[:], gated[:].rearrange("p c n -> p (c n)").rearrange("p (c n) -> p c n", c=KT), ACT.Copy
                                     ).then_inc(gated_high, 1)
                for t in range(SLOTS):
                    check_adj(b, t)

            def main(b, prepare_next):
                for t in range(RT):
                    width = N - t * P
                    act.wait_ge(scored, b * RT + t + 1)
                    if t >= 2:
                        act.wait_ge(alpha_ready, b * RT + t - 1)
                    scores = banks(2 * (t % 2), 2)[:, 0:width]
                    nc.scalar.activation(slopes[:, 2 * (t % 2), 0:width], scores, ACT.Tanh, scale=0.5 / SCALE)
                    nc.scalar.activation(slopes[:, 2 * (t % 2) + 1, 0:width], scores, ACT.Tanh, scale=0.5 * LEAK / SCALE
                                         ).then_inc(squashed, 1)
                    if 1 <= t <= RT - SLOTS:
                        check_adj(b, t + SLOTS - 1)
                for g in range(2):
                    act.wait_ge(x1_turned, b * 2 + g + 1)
                    nc.scalar.activation(x1_hi[:, 4 * g:4 * g + 4].rearrange("p t c q -> p (t c q)"), banks(2 * g, 2), ACT.Copy
                                         ).then_inc(x1_high, 1)
                act.wait_ge(ones_set, b + 1)
                for t in range(RT):
                    act.wait_ge(values_ready, b * RT + t + 1)
                    product = ps[:, 4 + t % 4, :]
                    nc.scalar.activation(values[:, t, :, 0:F], product[:, 0:D].rearrange("p (h f) -> p h f", h=H), ACT.Copy, scale=1 / SCALE)
                    nc.scalar.activation(sd[:, t], product[:, D:DX].rearrange("p (s h) -> p s h", s=2), ACT.Copy, scale=1 / SCALE
                                         ).then_inc(values_taken, 1)
                act.wait_ge(rows_ready, b + 1)
                nc.scalar.activation(src_rows[0:H, :], banks(0, 2)[0:H, :], ACT.Copy, scale=1 / SCALE).then_inc(rows_high, 1)
                for h in range(H):
                    act.wait_ge(src_spread, b * H + h + 1)
                    nc.scalar.activation(src_all[:, h, :], banks(SRC_BANKS[h], 2), ACT.Copy).then_inc(src_copied, 1)
                    if h == 1:
                        act.wait_ge(relative, b + 1)
                        nc.scalar.activation(exp_full[:], dst_rel[:], ACT.Exp, bias=log_scale[:])
                        nc.scalar.activation(exp_leak[:], dst_rel[:], ACT.Exp, bias=log_scale[:], scale=LEAK)
                        nc.scalar.activation(exp_src[:], src_rel[:], ACT.Exp, scale=1 - LEAK).then_inc(exps_ready, 1)
                act.wait_ge(full_ready, b + 1)
                nc.scalar.activation(step_rhs[:, 0, :, :, 0:F1].rearrange("p t h f -> p (t h) f"),
                                     prod_full[:].rearrange("p t h f -> p (t h) f"), ACT.Copy).then_inc(full_high, 1)
                act.wait_ge(leak_ready, b + 1)
                nc.scalar.activation(edge_rhs[:, 0], prod_leak[:], ACT.Copy).then_inc(leak_high, 1)
                prepare_next()
                act.wait_ge(negative_ready, b + 1)
                nc.scalar.activation(grown, grown, ACT.Exp).then_inc(grown_ready, 1)

            act.wait_ge(w_whole, 1)
            nc.scalar.activation(W_hi[:], W_ext[:], ACT.Copy, scale=SCALE).then_inc(w_split, 1)
            over_batches(act, prepare, main)

        @block.tensor
        def _(pe):
            pe.wait_ge(pool_consts, 1)
            pe.wait_ge(w_split, 3)
            for c in range(KT):
                last = nc.tensor.matmul(ps[:, 0, 0:D], ones[:], W_sq[:, c, 0:D], start=(c == 0), stop=(c == KT - 1))
            last.then_inc(norms_ready, 1)

            def main(b, prepare_next):
                def score(t):
                    if t == 0:
                        pe.wait_ge(cols_split, b + 1)
                        pe.wait_ge(gated_split, b + 1)
                        pe.wait_ge(bank_taken, b * (H * NG) + 1)
                    if t >= 2:
                        pe.wait_ge(squashed, b * RT + t - 1)
                    own = slice(t * P, (t + 1) * P)
                    scores = banks(2 * (t % 2), 2)
                    for start in range(t * P, N, BANK):
                        cut = slice(start, min(start + BANK, N))
                        dst = scores[:, cut.start - t * P:cut.stop - t * P]
                        terms = [(lhs, rhs, c) for lhs, rhs in ((gated_hi, cols_hi), (gated_hi, cols_lo), (gated_lo, cols_hi))
                                 for c in range(KT)]
                        for n, (lhs, rhs, c) in enumerate(terms):
                            last = nc.tensor.matmul(dst, lhs[:, c, own], rhs[:, c, cut], start=(n == 0), stop=(n == len(terms) - 1))
                    last.then_inc(scored, 1)

                def turn(t):
                    pe.wait_ge(alpha_ready, b * RT + t + 1)
                    if t >= 1:
                        pe.wait_ge(masked, b * RT + t)
                    for j in range(RT - 1 - t):
                        last = nc.tensor.transpose(banks(4, 2)[:, j * P:(j + 1) * P], alpha[:, t % 2, (j + 1) * P:(j + 2) * P], ident[:])
                    last.then_inc(turned, 1)

                def add_up(t):
                    pe.wait_ge(masked, b * RT + t + 1)
                    if t == 0:
                        pe.wait_ge(x_rows_in, b * 16 + 16)
                    if t >= 2:
                        pe.wait_ge(sum_taken, b * RT + t - 1)
                    for j in range(RT):
                        last = nc.tensor.matmul(ps[:, 6 + t % 2, 0:D], weights[:, j, t * P:(t + 1) * P], x_rows[:, j, :],
                                                start=(j == 0), stop=(j == RT - 1))
                    last.then_inc(summed, 1)

                for s in range(RT + 3):
                    if s < RT:
                        score(s)
                    if 0 <= s - 2 < RT - 1:
                        turn(s - 2)
                    if 0 <= s - 3:
                        add_up(s - 3)
                for t in range(RT):
                    pe.wait_ge(x1_ready, b * RT + t + 1)
                    if t == 0:
                        pe.wait_ge(squashed, b * RT + RT)
                    for c in range(KT):
                        last = nc.tensor.transpose(ps[:, t // 2, (t % 2 * KT + c) * P:(t % 2 * KT + c + 1) * P],
                                                   x1_rows[:, t, c * P:(c + 1) * P], ident[:])
                    if t % 4 == 3:
                        last.then_inc(x1_turned, 1)
                x1_pairs = ((x1_hi, W_hi), (x1_hi, W_lo), (x1_lo, W_hi))
                for t in range(RT):
                    if t % 4 == 0:
                        pe.wait_ge(x1_split, b * 2 + t // 4 + 1)
                    if t == 0:
                        pe.wait_ge(sum_taken, b * RT + RT)
                    if t >= 4:
                        pe.wait_ge(values_taken, b * RT + t - 3)
                    terms = [(lhs, rhs, c) for lhs, rhs in x1_pairs for c in range(KT)]
                    for n, (lhs, rhs, c) in enumerate(terms):
                        last = nc.tensor.matmul(ps[:, 4 + t % 4, 0:DX], lhs[:, t, c, :], rhs[:, c, :],
                                                start=(n == 0), stop=(n == len(terms) - 1))
                    last.then_inc(values_ready, 1)
                for half in range(2):
                    cut = slice(half * RT // 2, (half + 1) * RT // 2)
                    terms = [(rhs, lhs, c) for lhs, rhs in x1_pairs for c in range(KT)]
                    for n, (lhs, rhs, c) in enumerate(terms):
                        last = nc.tensor.matmul(ps[0:H, half, :], lhs[:, c, D:D + H], rhs[:, cut, c, :],
                                                start=(n == 0), stop=(n == len(terms) - 1))
                last.then_inc(rows_ready, 1)
                pe.wait_ge(rows_split, b + 1)
                for h in range(H):
                    if h == 1:
                        pe.wait_ge(values_taken, b * RT + RT)
                    if h == 3:
                        pe.wait_ge(src_copied, b * H + 1)
                    for half in range(2):
                        last = nc.tensor.matmul(ps[:, SRC_BANKS[h] + half, :], head_pick[:, h, :], src_rows[:, half * HN:(half + 1) * HN],
                                                start=True, stop=True)
                    last.then_inc(src_spread, 1)
                pe.wait_ge(src_copied, b * H + H)
                pe.wait_ge(rhs_ready, b + 1)
                for h in range(H):
                    pe.wait_ge(step_ready, b * H + h + 1)
                    if h >= 2:
                        pe.wait_ge(bank_taken, b * (H * NG) + (h - 1) * NG + 1)
                    for g, (t0, count) in enumerate(GROUPS):
                        bank = ps[:, h % 2 * 3 + g, :]
                        for t in range(count):
                            own = slice((t0 + t) * P, (t0 + t + 1) * P)
                            for j in range(RT):
                                for part in range(2):
                                    nc.tensor.matmul(bank[:, t * 2 * F1:(t + 1) * 2 * F1], step[:, h % 2, j, own], step_rhs[:, part, j, h, :],
                                                     start=(t == 0 and j == 0 and part == 0), stop=False, skip_group_check=True)
                                for part in range(2):
                                    last = nc.tensor.matmul(bank[:, t * 2 * F1 + F1:(t + 1) * 2 * F1], edge[:, j, own], edge_rhs[:, part, j, h, :],
                                                            start=False, stop=(j == RT - 1 and part == 1), skip_group_check=True)
                        last.then_inc(bank_done, 1)

            with pe.Fori(0, B - 1) as b:
                main(b, None)
            main(B - 1, None)

        @block.vector
        def _(dve):
            def constants():
                dve.wait_ge(constants_in, 80)
                nc.vector.memset(ones[:], 1.0)
                nc.vector.memset(minus_half[:], -0.5)
                nc.vector.memset(log_scale[:], LOG_VALUE_SCALE)
                nc.vector.memset(minus_one[:], -1.0)
                nc.vector.memset(worst[:], -1.0)
                nc.vector.memset(seen[:], -1.0)
                nc.vector.memset(limit[:, 0:RT], 0.0)
                for n, most in enumerate((SQUARES_MOST, RANGE_MOST, SHIFT_MOST, 0.0, W_SQ_MOST, W_NORM_MOST, GATE_SQ_MOST)):
                    at = CHECK_AT[n]
                    nc.vector.memset(limit[:, at:CHECK_AT[n + 1]], most)
                nc.vector.tensor_scalar(gate[:], gate_in[:, :, 0], SCALE, None, ALU.mult).then_inc(consts_made, 1)
                for c in range(KT):
                    for s in range(2):
                        nc.vector.tensor_tensor(wa_prod[:, c, s, :], W_ext[:, c, 0:D], a_all[:, s, :], ALU.mult)
                dve.drain()
                for c in range(KT):
                    for s in range(2):
                        nc.vector.reduce_sum(W_ext[:, c, D + s * H:D + (s + 1) * H], wa_prod[:, c, s, :].rearrange("p (h f) -> p h f", h=H), AX_X)
                dve.drain()
                nc.vector.tensor_tensor(gate_sq[:], gate_in[:, :, 0], gate_in[:, :, 0], ALU.mult)
                nc.vector.tensor_tensor(W_sq, W_ext[:], W_ext[:], ALU.mult).then_inc(w_whole, 1)
                dve.drain()
                nc.vector.tensor_reduce(worst[:, CHECK_AT[4]:CHECK_AT[4] + 1], W_sq, AX_XY, ALU.max)
                nc.vector.tensor_reduce(worst[:, CHECK_AT[6]:CHECK_AT[6] + 1], gate_sq[:], AX_X, ALU.max)
                dve.wait_ge(w_split, 1)
                nc.vector.scalar_tensor_tensor(W_lo[:], W_ext[:], SCALE, W_hi[:], ALU.mult, ALU.subtract).then_inc(w_split, 2)
                dve.wait_ge(norms_ready, 1)
                nc.vector.reduce_max(worst[:, CHECK_AT[5]:CHECK_AT[5] + 1], ps[:, 0, 0:D], AX_X).then_inc(bank_taken, 1)
                dve.drain()

            def gather_worst(at, end, latest):
                nc.vector.tensor_tensor(worst[:, at:end], worst[:, at:end], latest, ALU.max)

            def prepare(b):
                dve.wait_ge(x_cols_in, b * 16 + 16)
                for c in range(KT):
                    last = nc.vector.tensor_scalar(gated[:, c, :], x_cols[:, c, :], gate[:, c:c + 1], None, ALU.mult)
                last.then_inc(gated_ready, 1)

            def row_stats(t, rows):
                nc.vector.bn_stats(stats[:, t, :], rows[:, t, :])
                dve.drain()
                nc.vector.bn_aggr(moments[:, t, :], stats[:, t, :])

            def normalise(t, rows):
                return nc.vector.tensor_scalar(rows[:, t, :], rows[:, t, :], moments[:, t, 0:1], rstd[:, t:t + 1],
                                               ALU.subtract, ALU.mult)

            def main(b, prepare_next):
                def build_edge(t):
                    dve.wait_ge(adj_in[t % SLOTS], b * (RT // SLOTS * 16) + t // SLOTS * 16 + 16)
                    nc.vector.tensor_scalar(edge[:, t, :], adj_cols[:, t % SLOTS, :], 1.0, None, ALU.is_equal).then_inc(edge_built, 1)

                for t in range(SLOTS):
                    build_edge(t)

                def leak(t):
                    width = N - t * P
                    dve.wait_ge(squashed, b * RT + t + 1)
                    nc.vector.tensor_tensor(alpha[:, t % 2, 0:width], slopes[:, 2 * (t % 2), 0:width], slopes[:, 2 * (t % 2) + 1, 0:width],
                                            ALU.max).then_inc(alpha_ready, 1)

                def mask_turned(t):
                    dve.wait_ge(turned, b * (RT - 1) + t + 1)
                    nc.vector.scalar_tensor_tensor(
                        weights[:, t + 1:RT, t * P:(t + 1) * P],
                        banks(4, 2)[:, 0:(RT - 1 - t) * P].rearrange("p (j q) -> p j q", q=P),
                        1.0, edge[:, t + 1:RT, t * P:(t + 1) * P], ALU.add, ALU.mult).then_inc(masked, 1)

                def mask_own(t):
                    width = N - t * P
                    dve.wait_ge(alpha_ready, b * RT + t + 1)
                    last = nc.vector.scalar_tensor_tensor(weights[:, t, t * P:N], alpha[:, t % 2, 0:width], 1.0, edge[:, t, t * P:N],
                                                          ALU.add, ALU.mult)
                    if t == RT - 1:
                        last.then_inc(masked, 1)

                def take_sum(t):
                    if t == 0:
                        dve.wait_ge(biased, b + 1)
                    dve.wait_ge(summed, b * RT + t + 1)
                    nc.vector.scalar_tensor_tensor(x1_rows[:, t, :], ps[:, 6 + t % 2, 0:D], 0.5, x_bias[:, t, :],
                                                   ALU.mult, ALU.add).then_inc(sum_taken, 1)
                    dve.drain()
                    row_stats(t, x1_rows)
                    dve.drain()
                    nc.vector.tensor_scalar(var[:, t:t + 1], moments[:, t, 1:2], LN_EPS, None, ALU.add).then_inc(var_ready, 1)

                for s in range(RT + 5):
                    if s < RT:
                        leak(s)
                    if 0 <= s - 1 < RT - 1:
                        mask_turned(s - 1)
                    if s < RT:
                        mask_own(s)
                    if s == 0:
                        for t in range(SLOTS, RT):
                            build_edge(t)
                        dve.drain()
                    if 0 <= s - 4 < RT:
                        take_sum(s - 4)
                    if 0 <= s - 5:
                        dve.wait_ge(rstd_ready, b * RT + s - 4)
                        normalise(s - 5, x1_rows).then_inc(x1_ready, 1)
                nc.vector.memset(values[:, :, :, F:F1], 1.0).then_inc(ones_set, 1)
                for g in range(2):
                    dve.wait_ge(x1_high, b * 2 + g + 1)
                    half = slice(4 * g, 4 * g + 4)
                    nc.vector.tensor_tensor(x1_lo[:, half].rearrange("p t c q -> p (t c q)"), banks(2 * g, 2),
                                            x1_hi[:, half].rearrange("p t c q -> p (t c q)"), ALU.subtract).then_inc(x1_split, 1)
                dve.wait_ge(values_taken, b * RT + RT)
                nc.vector.tensor_scalar(dst_neg[:], sd[:, :, 1, :], -1.0, None, ALU.mult)
                nc.vector.reduce_max(peaks[:, 0, :], sd[:, :, 0, :].rearrange("p t h -> p h t"), AX_X)
                nc.vector.reduce_max(peaks[:, 1, :], sd[:, :, 1, :].rearrange("p t h -> p h t"), AX_X)
                dve.drain()
                nc.vector.reduce_max(peaks[:, 2, :], dst_neg[:].rearrange("p t h -> p h t"), AX_X).then_inc(peaks_ready, 1)
                dve.wait_ge(rows_high, b + 1)
                nc.vector.scalar_tensor_tensor(src_rows[32:32 + H, :], banks(0, 2)[0:H, :], 1 / SCALE, src_rows[0:H, :],
                                               ALU.mult, ALU.subtract).then_inc(rows_split, 1)

                def steps(h, tiles):
                    for t in tiles:
                        last = nc.vector.scalar_tensor_tensor(step[:, h % 2, t, :], src_all[:, h, :], dst_neg[:, t, h:h + 1], edge[:, t, :],
                                                              ALU.is_gt, ALU.mult)
                        if t == RT - 1:
                            last.then_inc(step_ready, 1)

                def take_head(h):
                    dve.drain()
                    sums = [ps[:, h % 2 * 3 + g, 0:count * 2 * F1].rearrange("p (t k f) -> p t k f", t=count, k=2)
                            for g, (t0, count) in enumerate(GROUPS)]
                    for g, (t0, count) in enumerate(GROUPS):
                        dve.wait_ge(bank_done, b * (H * NG) + h * NG + g + 1)
                        nc.vector.tensor_tensor(boosted[:, t0:t0 + count, :], sums[g][:, :, 0, :],
                                                exp_src[:, t0:t0 + count, h:h + 1].to_broadcast([P, count, F1]), ALU.mult)
                    dve.drain()
                    for g, (t0, count) in enumerate(GROUPS):
                        nc.vector.tensor_tensor(attended[:, t0:t0 + count, h, :], boosted[:, t0:t0 + count, :], sums[g][:, :, 1, :],
                                                ALU.add).then_inc(bank_taken, 1)

                dve.wait_ge(src_copied, b * H + 1)
                steps(0, range(0, 3))
                dve.wait_ge(tops_ready, b + 1)
                top = tops[:, 1:2, :].to_broadcast([P, RT, H])
                nc.vector.tensor_tensor(dst_rel[:], sd[:, :, 1, :], top, ALU.subtract)
                nc.vector.tensor_tensor(src_rel[:], sd[:, :, 0, :], top, ALU.add)
                dve.drain()
                nc.vector.tensor_scalar(src_rel[:], src_rel[:], SHIFT_MOST, None, ALU.min).then_inc(relative, 1)
                nc.vector.tensor_tensor(seen[:, CHECK_AT[1]:CHECK_AT[2]], tops[:, 2, :], tops[:, 1, :], ALU.add)
                nc.vector.tensor_tensor(seen[:, CHECK_AT[2]:CHECK_AT[3]], tops[:, 0, :], tops[:, 1, :], ALU.add)
                dve.drain()
                nc.vector.tensor_tensor(worst[:, 0:CHECK_AT[3]], worst[:, 0:CHECK_AT[3]], seen[:, 0:CHECK_AT[3]], ALU.max)
                steps(0, range(3, RT))
                dve.wait_ge(exps_ready, b + 1)
                nc.vector.tensor_tensor(prod_full[:], values[:], exp_full[:].rearrange("p t (h o) -> p t h o", o=1).to_broadcast([P, RT, H, F1]),
                                        ALU.mult).then_inc(full_ready, 1)
                dve.wait_ge(full_high, b + 1)
                nc.vector.tensor_tensor(step_rhs[:, 1, :, :, 0:F1], prod_full[:], step_rhs[:, 0, :, :, 0:F1], ALU.subtract)
                dve.wait_ge(leak_high, b + 1)
                nc.vector.tensor_tensor(edge_rhs[:, 1], prod_leak[:], edge_rhs[:, 0], ALU.subtract)
                dve.drain()
                for part in range(2):
                    last = nc.vector.tensor_scalar(step_rhs[:, part, :, :, F1:2 * F1], edge_rhs[:, part], -1.0, None, ALU.mult)
                last.then_inc(rhs_ready, 1)
                dve.wait_ge(src_copied, b * H + H)
                steps(1, range(RT))
                prepare_next()
                take_head(0)
                steps(2, range(RT))
                take_head(1)
                steps(3, range(RT))
                take_head(2)
                take_head(3)
                dve.drain()
                nc.vector.tensor_reduce(least[:], attended[:, :, :, F], AX_XY, ALU.min)
                nc.vector.tensor_scalar(inv_sum[:], attended[:, :, :, F], TINY, None, ALU.max)
                dve.drain()
                nc.vector.reciprocal(inv_sum[:], inv_sum[:])
                dve.drain()
                nc.vector.tensor_scalar(seen[:, CHECK_AT[3]:CHECK_AT[4]], least[:], TINY, None, ALU.is_le)
                nc.vector.tensor_tensor(heads[:, :, 0:F], heads[:, :, 0:F],
                                        inv_sum[:].rearrange("p t (h o) -> p (t h) o", o=1).to_broadcast([P, RT * H, F]), ALU.mult)
                dve.drain()
                nc.vector.tensor_scalar(grown, heads[:, :, 0:F], 0.0, None, ALU.min).then_inc(negative_ready, 1)
                dve.drain()
                gather_worst(CHECK_AT[3], CHECK_AT[4], seen[:, CHECK_AT[3]:CHECK_AT[4]])
                dve.wait_ge(grown_ready, b + 1)
                x1_heads = x1_rows[:].rearrange("p t (h f) -> p (t h) f", h=H)
                out_heads = out_rows.rearrange("p t (h f) -> p (t h) f", h=H)
                for half in range(2):
                    cut = slice(half * RT // 2, (half + 1) * RT // 2)
                    hcut = slice(cut.start * H, cut.stop * H)
                    nc.vector.scalar_tensor_tensor(out_heads[:, hcut], grown[:, hcut], -1.0, x1_heads[:, hcut], ALU.add, ALU.add)
                    dve.drain()
                    nc.vector.scalar_tensor_tensor(out_heads[:, hcut], heads[:, hcut, 0:F], 0.0, out_heads[:, hcut], ALU.max, ALU.add)
                    dve.drain()
                    for t in range(cut.start, cut.stop):
                        nc.vector.bn_stats(stats[:, t, :], out_rows[:, t, :])
                    dve.drain()
                    for t in range(cut.start, cut.stop):
                        nc.vector.bn_aggr(moments[:, t, :], stats[:, t, :])
                    dve.drain()
                    nc.vector.tensor_scalar(var[:, cut], moments[:, cut, 1], LN_EPS, None, ALU.add).then_inc(var1_ready, 1)
                for half in range(2):
                    dve.wait_ge(rstd1_ready, b * 2 + half + 1)
                    for t in range(half * RT // 2, (half + 1) * RT // 2):
                        last = normalise(t, out_rows)
                    last.then_inc(out_ready, 1)

            constants()
            over_batches(dve, prepare, main)
            dve.drain()
            nc.vector.tensor_tensor(limit[:], worst[:], limit[:], ALU.is_gt)
            dve.drain()
            nc.vector.reduce_max(beyond[:], limit[:], AX_X).then_inc(beyond_ready, 1)
            dve.wait_ge(beyond_reduced, 1)
            nc.vector.tensor_copy(flag_sb[:], beyond_any[0:1, :])


def general_path(nc, x, xT, adj, gates, bias, W, a_src, a_dst, out, flag_sb):
    B, N, D = x.shape
    H, F = a_src.shape
    KT, RT, TYPES = D // P, N // P, gates.shape[2]
    HN = N // 2

    with ExitStack() as ctx:
        def sb(name, shape, dt=F32):
            return ctx.enter_context(nc.sbuf_tensor("g_" + name, shape, dt))

        def ps(name, shape, dt=F32):
            return ctx.enter_context(nc.psum_tensor("g_" + name, shape, dt))

        def sem(name):
            return ctx.enter_context(nc.semaphore("g_" + name))

        h_rows = sb("h_rows", [P, RT, D])
        h_cols = sb("h_cols", [P, KT, N])
        adj_rows = sb("adj_rows", [P, N], I32)
        gate_cols = sb("gate_cols", [P, KT, TYPES])
        bias_all = sb("bias_all", [P, D])
        W_sb = sb("W_sb", [P, KT, D])
        a_all = sb("a_all", [P, 2, D])
        wa_prod = sb("wa_prod", [P, D])
        wa = sb("wa", [P, KT, 2, H])
        wa_wide = sb("wa_wide", [P, KT, H, P])
        ones = sb("ones", [P, P])
        ident = sb("ident", [P, P])
        gated = sb("gated", [P, KT, P])
        picked = sb("picked", [P, N])
        scores = sb("scores", [P, N])
        in_range = sb("in_range", [P, N])
        weights = sb("weights", [P, N])
        masked = sb("masked", [P, N])
        weights_T = sb("weights_T", [P, RT, P])
        row = sb("row", [P, D])
        stats = sb("stats", [P, 6])
        moments = sb("moments", [P, 2])
        var = sb("var", [P, 1])
        std = sb("std", [P, 1])
        x1_rows = sb("x1_rows", [P, RT, D])
        x1_cols = sb("x1_cols", [P, KT, N])
        values = sb("values", [P, RT, D])
        src = sb("src", [P, RT, H])
        dst_all = sb("dst_all", [P, H, N])
        mask = sb("mask", [P, N])
        penalty = sb("penalty", [P, N])
        row_max = sb("row_max", [P, 1])
        row_sum = sb("row_sum", [P, 1])
        attended = sb("attended", [P, D])
        negative = sb("negative", [P, D])
        grown = sb("grown", [P, D])

        score_ps = ps("score_ps", [P, N])
        turn_ps = ps("turn_ps", [P, N])
        row_ps = ps("row_ps", [P, 512])
        wide_ps = ps("wide_ps", [P, 512])

        flag_in = sem("flag_in")
        constants_in = sem("constants_in")
        batch_in = sem("batch_in")
        adj_in = sem("adj_in")
        adj_used = sem("adj_used")
        stored = sem("stored")
        ident_zero = sem("ident_zero")
        ident_ready = sem("ident_ready")
        folded = sem("folded")
        gated_ready = sem("gated_ready")
        scores_ready = sem("scores_ready")
        leaked = sem("leaked")
        squashed = sem("squashed")
        masked_ready = sem("masked_ready")
        turned = sem("turned")
        turned_copied = sem("turned_copied")
        summed = sem("summed")
        var_ready = sem("var_ready")
        std_ready = sem("std_ready")
        x1_ready = sem("x1_ready")
        x1_turned = sem("x1_turned")
        x1_whole = sem("x1_whole")
        values_ready = sem("values_ready")
        values_copied = sem("values_copied")
        dst_ready = sem("dst_ready")
        dst_copied = sem("dst_copied")
        exp_in = sem("exp_in")
        exp_out = sem("exp_out")
        exp_turned = sem("exp_turned")
        exp_copied = sem("exp_copied")
        head_summed = sem("head_summed")
        negative_ready = sem("negative_ready")
        grown_ready = sem("grown_ready")
        out_ready = sem("out_ready")
        batch_done = sem("batch_done")

        def sync_program(sp):
            sp.dma_start(gate_cols[:], gates).then_inc(constants_in, 16)
            sp.dma_start(bias_all[:], bias.partition_broadcast(P)).then_inc(constants_in, 16)
            sp.dma_start(W_sb[:], W.rearrange("(c p) n -> p c n", p=P)).then_inc(constants_in, 16)
            for s, a in enumerate((a_src, a_dst)):
                sp.dma_start(a_all[:, s, :], a.rearrange("h f -> (h f)").partition_broadcast(P)).then_inc(constants_in, 16)
            with sp.Fori(0, B) as b:
                sp.wait_ge(batch_done, b + 1)
                sp.dma_start(h_rows[:], x[bass.ds(b, 1)].rearrange("a (t p) d -> p (a t) d", p=P)).then_inc(batch_in, 16)
                sp.dma_start(h_cols[:], xT[bass.ds(b, 1)].rearrange("a (c p) n -> p (a c) n", p=P)).then_inc(batch_in, 16)
                with sp.Fori(0, RT) as t:
                    sp.wait_ge(adj_used, b * (2 * RT) + t + 1)
                    sp.dma_start(adj_rows[:], adj[bass.ds(b, 1), bass.ds(t * P, P)].rearrange("a p n -> p (a n)")
                                 ).then_inc(adj_in, 16)
                with sp.Fori(0, RT) as t:
                    sp.wait_ge(adj_used, b * (2 * RT) + t + RT + 1)
                    sp.dma_start(adj_rows[:], adj[bass.ds(b, 1), bass.ds(t * P, P)].rearrange("a p n -> p (a n)")
                                 ).then_inc(adj_in, 16)
                    sp.wait_ge(out_ready, b * RT + t + 1)
                    sp.dma_start(out[bass.ds(b, 1), bass.ds(t * P, P)].rearrange("a p n -> p (a n)"), row[:]
                                 ).then_inc(stored, 16)
            sp.wait_ge(stored, B * RT * 16)

        def gpsimd_program(pool):
            nc.gpsimd.memset(ident[:], 0.0).then_inc(ident_zero, 1)
            pool.wait_ge(ident_zero, 1)
            nc.gpsimd.affine_select(out=ident[:], in_=ident[:], compare_op=ALU.not_equal, fill=1.0,
                                    base=0, pattern=[[-1, P]], channel_multiplier=1).then_inc(ident_ready, 1)

        def scalar_program(act):
            with act.Fori(0, B) as b:
                with act.Fori(0, RT) as t:
                    act.wait_ge(leaked, b * RT + t + 1)
                    nc.scalar.activation(weights[:], scores[:], ACT.Sigmoid).then_inc(squashed, 1)
                    act.wait_ge(var_ready, b * (2 * RT) + t + 1)
                    nc.scalar.activation(std[:], var[:], ACT.Sqrt).then_inc(std_ready, 1)
                with act.Fori(0, RT) as t:
                    for h in range(H):
                        act.wait_ge(exp_in, (b * RT + t) * H + h + 1)
                        nc.scalar.activation(weights[:], scores[:], ACT.Exp, accum_out=row_sum[:]).then_inc(exp_out, 1)
                    act.wait_ge(negative_ready, b * RT + t + 1)
                    nc.scalar.activation(grown[:], negative[:], ACT.Exp).then_inc(grown_ready, 1)
                    act.wait_ge(var_ready, b * (2 * RT) + t + RT + 1)
                    nc.scalar.activation(std[:], var[:], ACT.Sqrt).then_inc(std_ready, 1)

        def tensor_program(pe):
            pe.wait_ge(ident_ready, 1)
            pe.wait_ge(folded, 1)
            with pe.Fori(0, B) as b:
                with pe.Fori(0, RT) as t:
                    n = b * RT + t
                    pe.wait_ge(batch_in, b * 32 + 32)
                    for k in range(TYPES):
                        pe.wait_ge(gated_ready, n * TYPES + k + 1)
                        for half in range(2):
                            cut = slice(half * HN, (half + 1) * HN)
                            for c in range(KT):
                                last = nc.tensor.matmul(score_ps[:, cut], gated[:, c, :], h_cols[:, c, cut],
                                                        start=(c == 0), stop=(c == KT - 1))
                        last.then_inc(scores_ready, 1)
                    pe.wait_ge(masked_ready, n + 1)
                    for j in range(RT):
                        last = nc.tensor.transpose(turn_ps[:, j * P:(j + 1) * P], masked[:, j * P:(j + 1) * P], ident[:])
                    last.then_inc(turned, 1)
                    pe.wait_ge(turned_copied, n + 1)
                    for j in range(RT):
                        last = nc.tensor.matmul(row_ps[:, 0:D], weights_T[:, j, :], h_rows[:, j, :],
                                                start=(j == 0), stop=(j == RT - 1))
                    last.then_inc(summed, 1)
                    pe.wait_ge(x1_ready, n + 1)
                    for c in range(KT):
                        last = nc.tensor.transpose(wide_ps[:, c * P:(c + 1) * P], row[:, c * P:(c + 1) * P], ident[:])
                    last.then_inc(x1_turned, 1)
                pe.wait_ge(x1_whole, b + 1)
                for t in range(RT):
                    if t >= 1:
                        pe.wait_ge(values_copied, b * RT + t)
                    for c in range(KT):
                        nc.tensor.matmul(row_ps[:, 0:D], x1_cols[:, c, t * P:(t + 1) * P], W_sb[:, c, :],
                                         start=(c == 0), stop=(c == KT - 1))
                    for c in range(KT):
                        last = nc.tensor.matmul(wide_ps[:, 0:H], x1_cols[:, c, t * P:(t + 1) * P], wa[:, c, 0, :],
                                                start=(c == 0), stop=(c == KT - 1))
                    last.then_inc(values_ready, 1)
                pe.wait_ge(values_copied, b * RT + RT)
                for n in range(2 * H):
                    cut = slice(n % 2 * HN, (n % 2 + 1) * HN)
                    if n >= 1:
                        pe.wait_ge(dst_copied, b * (2 * H) + n)
                    for c in range(KT):
                        last = nc.tensor.matmul(wide_ps[:, 0:HN], wa_wide[:, c, n // 2, :], x1_cols[:, c, cut],
                                                start=(c == 0), stop=(c == KT - 1))
                    last.then_inc(dst_ready, 1)
                with pe.Fori(0, RT) as t:
                    n = b * RT + t
                    for h in range(H):
                        pe.wait_ge(exp_out, n * H + h + 1)
                        for j in range(RT):
                            last = nc.tensor.transpose(turn_ps[:, j * P:(j + 1) * P], weights[:, j * P:(j + 1) * P], ident[:])
                        last.then_inc(exp_turned, 1)
                        pe.wait_ge(exp_copied, n * H + h + 1)
                        for j in range(RT):
                            last = nc.tensor.matmul(row_ps[:, 0:F], weights_T[:, j, :], values[:, j, h * F:(h + 1) * F],
                                                    start=(j == 0), stop=(j == RT - 1))
                        last.then_inc(head_summed, 1)

        def vector_program(dve):
            def std_of_row(nth):
                nc.vector.bn_stats(stats[:], row[:])
                dve.drain()
                nc.vector.bn_aggr(moments[:], stats[:])
                dve.drain()
                nc.vector.tensor_scalar_add(var[:], moments[:, 1:2], LN_EPS).then_inc(var_ready, 1)
                dve.wait_ge(std_ready, nth)
                nc.vector.reciprocal(var[:], std[:])
                dve.drain()

            nc.vector.memset(stats[:], 0.0).then_inc(batch_done, 1)
            nc.vector.memset(row_max[:], 0.0).then_inc(adj_used, 1)
            dve.wait_ge(constants_in, 80)
            nc.vector.memset(ones[:], 1.0)
            for c in range(KT):
                for s in range(2):
                    dve.drain()
                    nc.vector.tensor_tensor(wa_prod[:], W_sb[:, c, :], a_all[:, s, :], ALU.mult)
                    dve.drain()
                    nc.vector.reduce_sum(wa[:, c, s, :], wa_prod[:].rearrange("p (h f) -> p h f", h=H), AX_X)
            dve.drain()
            for c in range(KT):
                for h in range(H):
                    last = nc.vector.tensor_scalar(wa_wide[:, c, h, :], ones[:], wa[:, c, 1, h:h + 1], None, ALU.mult)
            last.then_inc(folded, 1)
            dve.drain()

            with dve.Fori(0, B) as b:
                with dve.Fori(0, RT) as t:
                    n = b * RT + t
                    dve.wait_ge(batch_in, b * 32 + 32)
                    dve.wait_ge(adj_in, (b * (2 * RT) + t) * 16 + 16)
                    for k in range(TYPES):
                        for c in range(KT):
                            last = nc.vector.tensor_scalar(gated[:, c, :], h_cols[:, c, bass.ds(t * P, P)],
                                                           gate_cols[:, c, k:k + 1], None, ALU.mult)
                        last.then_inc(gated_ready, 1)
                        dve.wait_ge(scores_ready, n * TYPES + k + 1)
                        dst = scores if k else picked
                        nc.vector.scalar_tensor_tensor(dst[:], adj_rows[:], float(k + 1), score_ps[:],
                                                       ALU.is_equal, ALU.mult)
                        dve.drain()
                        if k:
                            nc.vector.tensor_tensor(picked[:], picked[:], scores[:], ALU.add)
                            dve.drain()
                    nc.vector.scalar_tensor_tensor(scores[:], picked[:], LEAK, picked[:], ALU.mult, ALU.max).then_inc(leaked, 1)
                    nc.vector.tensor_scalar(in_range[:], adj_rows[:], 1.0, None, ALU.is_ge)
                    dve.drain()
                    nc.vector.scalar_tensor_tensor(penalty[:], adj_rows[:], float(TYPES), in_range[:],
                                                   ALU.is_le, ALU.mult).then_inc(adj_used, 1)
                    dve.drain()
                    dve.wait_ge(squashed, n + 1)
                    nc.vector.tensor_tensor(masked[:], weights[:], penalty[:], ALU.mult).then_inc(masked_ready, 1)
                    dve.wait_ge(turned, n + 1)
                    nc.vector.tensor_copy(weights_T[:].rearrange("p t q -> p (t q)"), turn_ps[:]).then_inc(turned_copied, 1)
                    dve.wait_ge(summed, n + 1)
                    nc.vector.tensor_tensor(row[:], row_ps[:, 0:D], bias_all[:], ALU.add)
                    dve.drain()
                    nc.vector.tensor_tensor(row[:], row[:], h_rows[:, bass.ds(t, 1), :].rearrange("p a d -> p (a d)"), ALU.add)
                    dve.drain()
                    std_of_row(b * (2 * RT) + t + 1)
                    nc.vector.tensor_scalar(row[:], row[:], moments[:, 0:1], var[:], ALU.subtract, ALU.mult).then_inc(x1_ready, 1)
                    dve.drain()
                    nc.vector.tensor_copy(x1_rows[:, bass.ds(t, 1), :].rearrange("p a d -> p (a d)"), row[:])
                    dve.wait_ge(x1_turned, n + 1)
                    nc.vector.tensor_copy(x1_cols[:, :, bass.ds(t * P, P)], wide_ps[:, 0:D].rearrange("p (c q) -> p c q", c=KT))
                    dve.drain()
                nc.vector.memset(stats[:], 0.0).then_inc(x1_whole, 1)
                for t in range(RT):
                    dve.wait_ge(values_ready, b * RT + t + 1)
                    nc.vector.tensor_copy(src[:, t, :], wide_ps[:, 0:H])
                    dve.drain()
                    nc.vector.tensor_copy(values[:, t, :], row_ps[:, 0:D]).then_inc(values_copied, 1)
                for m in range(2 * H):
                    dve.wait_ge(dst_ready, b * (2 * H) + m + 1)
                    nc.vector.tensor_copy(dst_all[:, m // 2, m % 2 * HN:(m % 2 + 1) * HN], wide_ps[:, 0:HN]).then_inc(dst_copied, 1)
                dve.drain()
                with dve.Fori(0, RT) as t:
                    n = b * RT + t
                    dve.wait_ge(adj_in, (b * (2 * RT) + t) * 16 + RT * 16 + 16)
                    nc.vector.tensor_scalar(mask[:], adj_rows[:], 0.0, None, ALU.is_gt).then_inc(adj_used, 1)
                    dve.drain()
                    nc.vector.tensor_scalar(penalty[:], mask[:], -NEG_INF, NEG_INF, ALU.mult, ALU.add)
                    dve.drain()
                    for h in range(H):
                        nc.vector.tensor_scalar(picked[:], dst_all[:, h, :], src[:, bass.ds(t, 1), h:h + 1].rearrange("p a h -> p (a h)"),
                                                None, ALU.add)
                        dve.drain()
                        nc.vector.scalar_tensor_tensor(scores[:], picked[:], LEAK, picked[:], ALU.mult, ALU.max)
                        dve.drain()
                        nc.vector.tensor_tensor(picked[:], scores[:], mask[:], ALU.mult)
                        dve.drain()
                        nc.vector.tensor_tensor(scores[:], picked[:], penalty[:], ALU.add)
                        dve.drain()
                        nc.vector.reduce_max(row_max[:], scores[:], AX_X)
                        dve.drain()
                        nc.vector.tensor_scalar(scores[:], scores[:], row_max[:], None, ALU.subtract).then_inc(exp_in, 1)
                        dve.wait_ge(exp_turned, n * H + h + 1)
                        nc.vector.tensor_copy(weights_T[:].rearrange("p t q -> p (t q)"), turn_ps[:]).then_inc(exp_copied, 1)
                        nc.vector.reciprocal(row_max[:], row_sum[:])
                        dve.drain()
                        dve.wait_ge(head_summed, n * H + h + 1)
                        nc.vector.tensor_scalar(attended[:, h * F:(h + 1) * F], row_ps[:, 0:F], row_max[:], None, ALU.mult)
                        dve.drain()
                    nc.vector.tensor_scalar(negative[:], attended[:], 0.0, None, ALU.min).then_inc(negative_ready, 1)
                    dve.wait_ge(grown_ready, n + 1)
                    nc.vector.tensor_scalar(grown[:], grown[:], 1.0, None, ALU.subtract)
                    dve.drain()
                    nc.vector.scalar_tensor_tensor(attended[:], attended[:], 0.0, grown[:], ALU.max, ALU.add)
                    dve.drain()
                    nc.vector.tensor_tensor(row[:], attended[:], x1_rows[:, bass.ds(t, 1), :].rearrange("p a d -> p (a d)"), ALU.add)
                    dve.drain()
                    std_of_row(b * (2 * RT) + t + RT + 1)
                    nc.vector.tensor_scalar(row[:], row[:], moments[:, 0:1], var[:], ALU.subtract, ALU.mult).then_inc(out_ready, 1)
                    dve.drain()
                    dve.wait_ge(stored, n * 16 + 16)
                nc.vector.memset(stats[:], 0.0).then_inc(batch_done, 1)
                dve.drain()

        block = ctx.enter_context(nc.Block())

        def when_flagged(eng, program):
            raw = eng.value_load(flag_sb[0:1, 0:1])
            with eng.If(raw > 0):
                program(eng)

        @block.sync
        def _(sp):
            when_flagged(sp, sync_program)

        @block.gpsimd
        def _(pool):
            when_flagged(pool, gpsimd_program)

        @block.scalar
        def _(act):
            when_flagged(act, scalar_program)

        @block.tensor
        def _(pe):
            when_flagged(pe, tensor_program)

        @block.vector
        def _(dve):
            when_flagged(dve, vector_program)


def build(nc, x, xT, adj, adjT, gates, bias, W, a_src, a_dst, out):
    with nc.sbuf_tensor("flag_sb", [1, 1], I32) as flag_sb:
        fast_path(nc, x, xT, adjT, gates, bias, W, a_src, a_dst, out, flag_sb)
        general_path(nc, x, xT, adj, gates, bias, W, a_src, a_dst, out, flag_sb)


def kernel(x, adj, L0_gnn_a0, L0_gnn_a1, L0_gnn_a2, L0_gnn_a3, L0_gnn_bias, L1_gnn_W, L1_gnn_a_src, L1_gnn_a_dst):
    import numpy as np
    import concourse.bacc as bacc
    from concourse.bass_utils import run_bass_kernel_spmd

    x, adj = np.asarray(x), np.asarray(adj)
    arrays = {
        "x": x,
        "xT": np.ascontiguousarray(x.transpose(0, 2, 1)),
        "adj": adj,
        "adjT": np.ascontiguousarray(adj.transpose(0, 2, 1)),
        "gates": np.ascontiguousarray(np.stack([np.asarray(a).reshape(-1, P).T for a in
                                                (L0_gnn_a0, L0_gnn_a1, L0_gnn_a2, L0_gnn_a3)], axis=2)),
        "bias": np.asarray(L0_gnn_bias),
        "W": np.asarray(L1_gnn_W),
        "a_src": np.asarray(L1_gnn_a_src),
        "a_dst": np.asarray(L1_gnn_a_dst),
    }
    nc = bacc.Bacc("TRN2", target_bir_lowering=False, num_devices=1)
    args = {n: nc.dram_tensor("in_" + n, a.shape, mybir.dt.from_np(a.dtype), kind="ExternalInput").ap()
            for n, a in arrays.items()}
    out = nc.dram_tensor("out", x.shape, F32, kind="ExternalOutput").ap()
    build(nc, **args, out=out)
    r = run_bass_kernel_spmd(nc, [{"in_" + n: a for n, a in arrays.items()}], core_ids=[0])
    return r.results[0]["out"]
```

```python
import math
from contextlib import ExitStack

import concourse.bass as bass
from concourse import mybir

P = 128
ALU = mybir.AluOpType
ACT = mybir.ActivationFunctionType
AX_X = mybir.AxisListType.X
AX_XY = mybir.AxisListType.XY
BF16 = mybir.dt.bfloat16
F16 = mybir.dt.float16
F32 = mybir.dt.float32
I32 = mybir.dt.int32

LEAK = 0.2
LN_EPS = 1e-5
NEG_INF = -1e9


def fast_path(nc, x, xT, adjT, gates, bias, W, a_src, a_dst, out, flag_sb):
    B, N, D = x.shape
    H, F = a_src.shape
    KT, RT = D // P, N // P
    HN = N // 2
    F1 = F + 1
    DX = D + 2 * H
    BANK = 512
    COMPARED = (2, 4, 6, 9, 15, 22)
    LIFTED = [n for n in range(H * RT) if n not in COMPARED]
    NL = len(LIFTED)
    STEEP = 2.0 ** 30
    RING = 4
    RESTED = tuple(h * RT + t for h in range(1, H) for t in ((1, 3, 5, 7) if h == H - 1 else (2, 4, 7)))
    NR = len(RESTED)
    REST_RING = 4
    SCALE = 64.0
    LOG_VALUE_SCALE = math.log(512.0)
    CHECK_AT = [RT, RT + 1, RT + 1 + H, RT + 1 + 2 * H]
    CHECK_AT += [CHECK_AT[-1] + n for n in (1, 2, 3, 4)]
    CHECKS = CHECK_AT[-1]
    SQUARES_MOST, RANGE_MOST, SHIFT_MOST = 2.0 ** 18, 14.0, 60.0
    TINY = 1e-6
    W_SQ_MOST, W_NORM_MOST, GATE_SQ_MOST = 900.0 ** 2, 60.0, 1.9 ** 2

    with ExitStack() as ctx:
        def sb(name, shape, dt=F32):
            return ctx.enter_context(nc.sbuf_tensor(name, shape, dt))

        def sem(name):
            return ctx.enter_context(nc.semaphore(name))

        x_rows = sb("x_rows", [P, RT, D])
        x_cols = sb("x_cols", [P, KT, N])
        adj_cols = sb("adj_cols", [P, RT, N], I32)
        edge = sb("edge", [P, RT, N], F16)
        gate_in = sb("gate_in", [P, KT, 4])
        gate = sb("gate", [P, KT])
        bias_all = sb("bias_all", [P, D])
        W_ext = sb("W_ext", [P, KT, DX])
        W_hi = sb("W_hi", [P, KT, DX], F16)
        W_lo = sb("W_lo", [P, KT, DX], F16)
        ones = sb("ones", [P, P])
        ident = sb("ident", [P, P])
        minus_half = sb("minus_half", [P, RT])
        log_scale = sb("log_scale", [P, 1])
        minus_one = sb("minus_one", [P, 1])
        head_pick = sb("head_pick", [64, H, P], F16)
        cols_hi = sb("cols_hi", [P, KT, N], F16)
        cols_lo = sb("cols_lo", [P, KT, N], F16)
        gated_hi = sb("gated_hi", [P, KT, N], F16)
        gated_lo = sb("gated_lo", [P, KT, N], F16)
        x_bias = sb("x_bias", [P, RT, D])
        alpha = sb("alpha", [P, 2, N])
        weights = sb("weights", [P, RT, N])
        stats = sb("stats", [P, RT, 6])
        moments = sb("moments", [P, RT, 2])
        var = sb("var", [P, RT])
        rstd = sb("rstd", [P, RT])
        x1_rows = sb("x1_rows", [P, RT, D])
        x1_hi = sb("x1_hi", [P, RT, KT, P], F16)
        x1_lo = sb("x1_lo", [P, RT, KT, P], F16)
        stats1 = sb("stats1", [P, RT, 6])
        moments1 = sb("moments1", [P, RT, 2])
        var1 = sb("var1", [P, RT])
        rstd1 = sb("rstd1", [P, RT])
        shift1 = sb("shift1", [P, RT])
        zeros = sb("zeros", [P, RT])
        values = sb("values", [P, RT, H, F1])
        sd = sb("sd", [P, RT, 2, H])
        peaks = sb("peaks", [P, 3, H])
        own_peaks = sb("own_peaks", [P, 3, H])
        tops = sb("tops", [P, 3, H])
        dst_neg = sb("dst_neg", [P, RT, H])
        dst_steep = sb("dst_steep", [P, RT, H])
        dst_rel = sb("dst_rel", [P, RT, H])
        src_rel = sb("src_rel", [P, RT, H])
        exp_full = sb("exp_full", [P, RT, H])
        exp_leak = sb("exp_leak", [P, RT, H])
        exp_src = sb("exp_src", [P, RT, H])
        prod_full = sb("prod_full", [P, RT, H, F1])
        prod_leak = sb("prod_leak", [P, RT, H, F1])
        step_rhs = sb("step_rhs", [P, 2, RT, H, 2 * F1], F16)
        edge_rhs = sb("edge_rhs", [P, 2, RT, H, F1], F16)
        src_rows = sb("src_rows", [64, N], F16)
        boosted = sb("boosted", [P, RT, F1])
        inv_sum = sb("inv_sum", [P, RT, H])
        least = sb("least", [P, 1])
        gate_sq = sb("gate_sq", [P, KT])
        seen = sb("seen", [P, CHECKS])
        worst = sb("worst", [P, CHECKS])
        limit = sb("limit", [P, CHECKS])
        beyond = sb("beyond", [P, 1])
        beyond_any = sb("beyond_any", [P, 1])

        rest = [part[:].rearrange("p t c q -> p (t c q)")[:, at * N:(at + 1) * N] for part in (x1_hi, x1_lo) for at in range(2)]

        def leak_product(h):
            return boosted[:] if h == 0 else prod_leak[:, :, h, :]

        src_all = weights[:, 0:H, :]
        step = weights[:, H:2 * H, :].bitcast(F16).rearrange("p t (u n) -> p (t u) n", u=2)
        above = alpha[:].bitcast(BF16).rearrange("p t (u n) -> p (t u) n", u=2)
        flat = weights[:].rearrange("p t n -> p (t n)")
        W_sq = flat[:, 0:KT * DX].rearrange("p (c n) -> p c n", c=KT)
        a_all = flat[:, N:N + 2 * D].rearrange("p (s n) -> p s n", s=2)
        wa_prod = flat[:, 2 * N:2 * N + KT * 2 * D].rearrange("p (c s n) -> p c s n", c=KT, s=2)
        unused = step_rhs[:, 0].rearrange("p t h f -> p (t h f)")[:, 0:KT * N]
        attended = prod_full
        heads = attended[:].rearrange("p t h f -> p (t h) f")
        grown = values[:].rearrange("p t h f -> p (t h f)")[:, 0:RT * D].rearrange("p (m f) -> p m f", f=F)
        out_rows = prod_leak[:].rearrange("p t h f -> p (t h f)")[:, 0:RT * D].rearrange("p (t d) -> p t d", d=D)

        ps = ctx.enter_context(nc.psum_tensor("ps", [P, 8, BANK], F32))

        def banks(first, count):
            return ps[:, first:first + count, :].rearrange("p b n -> p (b n)")

        def score_banks(t):
            return banks(6 if t == 0 else 2 * ((t + 1) % 2), 2)

        SRC_BANKS = (0, 2, 4, 4)
        GROUPS = [(g * 3, min(3, RT - g * 3)) for g in range((RT + 2) // 3)]
        NG = len(GROUPS)

        constants_in = sem("constants_in")
        x_cols_in = sem("x_cols_in")
        x_rows_in = sem("x_rows_in")
        adj_in = [sem(f"adj_in{n}") for n in range(RT)]
        stored = sem("stored")
        out_free = sem("out_free")
        consts_made = sem("consts_made")
        pool_consts = sem("pool_consts")
        w_whole = sem("w_whole")
        w_split = sem("w_split")
        norms_ready = sem("norms_ready")
        cols_high = sem("cols_high")
        cols_split = sem("cols_split")
        gated_high = sem("gated_high")
        gated_split = sem("gated_split")
        biased = sem("biased")
        x_checked = sem("x_checked")
        edge_built = sem("edge_built")
        adj_checked = sem("adj_checked")
        scored = sem("scored")
        squashed = sem("squashed")
        alpha_ready = sem("alpha_ready")
        turned = sem("turned")
        masked = sem("masked")
        summed = sem("summed")
        sum_taken = sem("sum_taken")
        var_ready = sem("var_ready")
        rstd_ready = sem("rstd_ready")
        x1_ready = sem("x1_ready")
        x1_turned = sem("x1_turned")
        x1_high = sem("x1_high")
        x1_split = sem("x1_split")
        ones_set = sem("ones_set")
        rows_ready = sem("rows_ready")
        values_ready = sem("values_ready")
        sd_ready = sem("sd_ready")
        values_taken = sem("values_taken")
        rows_high = sem("rows_high")
        rows_split = sem("rows_split")
        src_spread = sem("src_spread")
        src_copied = sem("src_copied")
        peaks_ready = sem("peaks_ready")
        tops_ready = sem("tops_ready")
        relative = sem("relative")
        exps_ready = sem("exps_ready")
        full_ready = sem("full_ready")
        leak_ready = sem("leak_ready")
        pool_full_ready = sem("pool_full_ready")
        full_high = sem("full_high")
        leak_high = sem("leak_high")
        pool_split = sem("pool_split")
        rhs_ready = sem("rhs_ready")
        above_ready = sem("above_ready")
        step_ready = sem("step_ready")
        step_used = sem("step_used")
        rest_ready = sem("rest_ready")
        bank_taken = sem("bank_taken")
        inverted = sem("inverted")
        divided = sem("divided")
        negative_ready = sem("negative_ready")
        grown_ready = sem("grown_ready")
        var1_ready = sem("var1_ready")
        shift1_ready = sem("shift1_ready")
        out_ready = sem("out_ready")
        beyond_ready = sem("beyond_ready")
        beyond_reduced = sem("beyond_reduced")

        def over_batches(eng, prepare, starts, main, finish, ends):
            for part in range(starts):
                prepare(0, part)
            main(0, lambda part: prepare(1, part), lambda part: None)
            with eng.Fori(1, B - 1) as b:
                main(b, lambda part: prepare(b + 1, part), lambda part: finish(b - 1, part))
            main(B - 1, lambda part: None, lambda part: finish(B - 2, part))
            for part in range(ends):
                finish(B - 1, part)

        def later(b):
            return not isinstance(b, int) or b >= 1

        def nothing(*_):
            pass

        block = ctx.enter_context(nc.Block())

        @block.sync
        def _(sp):
            sp.dma_start(gate_in[:], gates).then_inc(constants_in, 16)
            sp.dma_start(bias_all[:], bias.partition_broadcast(P)).then_inc(constants_in, 16)
            sp.dma_start(W_ext[:, :, 0:D], W.rearrange("(c p) n -> p c n", p=P)).then_inc(constants_in, 16)
            for s, a in enumerate((a_src, a_dst)):
                sp.dma_start(a_all[:, s, :], a.rearrange("h f -> (h f)").partition_broadcast(P)).then_inc(constants_in, 16)

            def prepare(b, part):
                if part == 0:
                    load_cols(b)
                else:
                    load_rest(b)

            def load_cols(b):
                if later(b):
                    sp.wait_ge(cols_split, b * KT)
                    sp.wait_ge(gated_split, b * KT)
                    sp.wait_ge(x_checked, b)
                sp.dma_start(x_cols[:], xT[bass.ds(b, 1)].rearrange("a (c p) n -> p (a c) n", p=P)).then_inc(x_cols_in, 16)

            def load_rest(b):
                for t in range(RT):
                    if later(b):
                        sp.wait_ge(edge_built, b * RT - RT + t + 1)
                        sp.wait_ge(adj_checked, b * RT - RT + t + 1)
                    sp.dma_start(adj_cols[:, t, :], adjT[bass.ds(b, 1), t * P:(t + 1) * P].rearrange("a p n -> p (a n)")
                                 ).then_inc(adj_in[t], 16)
                if later(b):
                    sp.wait_ge(summed, b * RT)
                sp.dma_start(x_rows[:], x[bass.ds(b, 1)].rearrange("a (t p) d -> p (a t) d", p=P)).then_inc(x_rows_in, 16)

            def main(b, prepare_next, finish_last):
                prepare_next(0)
                finish_last(0)
                prepare_next(1)

            def finish(b, _):
                for half in range(2):
                    cut = slice(half * RT // 2, (half + 1) * RT // 2)
                    sp.wait_ge(out_ready, b * RT + (half + 1) * RT // 2)
                    sp.dma_start(out[bass.ds(b, 1)].rearrange("a (t p) d -> p (a t) d", p=P)[:, cut, :], out_rows[:, cut, :]
                                 ).then_inc(stored, 16)
                sp.wait_ge(stored, b * 32 + 32)
                sp.sem_inc(out_free, 1)

            sp.sem_inc(out_free, 1)
            over_batches(sp, prepare, 2, main, finish, 1)
            sp.wait_ge(stored, B * 32)

        @block.gpsimd
        def _(pool):
            nc.gpsimd.memset(ident[:], 0.0)
            nc.gpsimd.memset(head_pick[:], 0.0)
            pool.drain()
            nc.gpsimd.affine_select(out=ident[:], in_=ident[:], compare_op=ALU.not_equal, fill=1.0,
                                    base=0, pattern=[[-1, P]], channel_multiplier=1)
            for part in range(2):
                pool.drain()
                block_of = head_pick[32 * part:32 * part + 32]
                nc.gpsimd.affine_select(out=block_of, in_=block_of, compare_op=ALU.not_equal, fill=1.0,
                                        base=0, pattern=[[-1, H], [0, P]], channel_multiplier=1)
            pool.drain()
            nc.gpsimd.memset(src_rows[:], 0.0).then_inc(pool_consts, 1)
            pool.wait_ge(constants_in, 80)
            pool.wait_ge(consts_made, 1)

            def prepare(b, part):
                pool.wait_ge(cols_high, b + 1)
                nc.gpsimd.tensor_tensor(cols_lo[:, part, :], x_cols[:, part, :], cols_hi[:, part, :], ALU.subtract).then_inc(cols_split, 1)

            def add_bias(b):
                pool.wait_ge(x_rows_in, b * 16 + 16)
                nc.gpsimd.tensor_tensor(x_bias[:], x_rows[:], bias_all[:].rearrange("p (a d) -> p a d", a=1).to_broadcast([P, RT, D]),
                                        ALU.add).then_inc(biased, 1)

            def main(b, prepare_next, finish_last):
                add_bias(b)
                for t in range(RT):
                    pool.wait_ge(var_ready, b * RT + t + 1)
                    nc.gpsimd.tensor_tensor(rstd[:, t:t + 1], var[:, t:t + 1], minus_half[:, t:t + 1], ALU.pow).then_inc(rstd_ready, 1)
                    if t == 2:
                        finish_last(0)
                    if t == 5:
                        prepare_next(0)
                    if t == 7:
                        finish_last(1)
                        prepare_next(1)
                pool.wait_ge(peaks_ready, b + 1)
                nc.gpsimd.tensor_tensor(own_peaks[:], peaks[:], ones[:, 0:3 * H].rearrange("p (k h) -> p k h", k=3), ALU.mult)
                pool.drain()
                nc.gpsimd.partition_all_reduce(tops[:].rearrange("p k h -> p (k h)"), own_peaks[:].rearrange("p k h -> p (k h)"),
                                               P, bass.bass_isa.ReduceOp.max).then_inc(tops_ready, 1)
                pool.wait_ge(exps_ready, b + 1)

                def weigh(h):
                    if h == 1:
                        pool.wait_ge(out_free, b + 1)
                    by_leak = exp_leak[:, :, h:h + 1].to_broadcast([P, RT, F1])
                    nc.gpsimd.tensor_tensor(leak_product(h), values[:, :, h, :], by_leak, ALU.mult).then_inc(leak_ready, 1)
                    if h >= 1:
                        by_full = exp_full[:, :, h:h + 1].to_broadcast([P, RT, F1])
                        nc.gpsimd.tensor_tensor(prod_full[:, :, h, :], values[:, :, h, :], by_full, ALU.mult).then_inc(pool_full_ready, 1)

                def split_full(h):
                    pool.wait_ge(full_high, b * H + h + 1)
                    nc.gpsimd.tensor_tensor(step_rhs[:, 1, :, h, 0:F1], prod_full[:, :, h, :], step_rhs[:, 0, :, h, 0:F1], ALU.subtract
                                            ).then_inc(pool_split, 1)

                def split_leak(h):
                    pool.wait_ge(leak_high, b * H + h + 1)
                    nc.gpsimd.tensor_tensor(edge_rhs[:, 1, :, h, :], prod_leak[:, :, h, :], edge_rhs[:, 0, :, h, :], ALU.subtract
                                            ).then_inc(pool_split, 1)

                def make_rest(n):
                    k = RESTED.index(n)
                    pool.wait_ge(step_ready, b * (H * RT) + n + 1)
                    if k >= REST_RING:
                        pool.wait_ge(step_used, b * (H * RT) + RESTED[k - REST_RING] + 1)
                    nc.gpsimd.tensor_tensor(rest[k % REST_RING], edge[:, n % RT, :], step[:, n % RT, :], ALU.subtract).then_inc(rest_ready, 1)

                def divide(h):
                    pool.wait_ge(inverted, b + 1)
                    nc.gpsimd.tensor_tensor(attended[:, :, h, 0:F], attended[:, :, h, 0:F],
                                            inv_sum[:, :, h:h + 1].to_broadcast([P, RT, F]), ALU.mult).then_inc(divided, 1)

                weigh(0)
                for h in range(H):
                    if h + 1 < H:
                        weigh(h + 1)
                    for t in range(RT):
                        if h * RT + t in RESTED:
                            make_rest(h * RT + t)
                        if h + 1 < H and t == 5:
                            split_full(h + 1)
                        if h + 1 < H and t == 6:
                            split_leak(h + 1)
                divide(H - 1)

            def finish(b, half):
                cut = slice(half * RT // 2, (half + 1) * RT // 2)
                pool.wait_ge(var1_ready, b * RT + (half + 1) * RT // 2)
                nc.gpsimd.tensor_tensor(rstd1[:, cut], var1[:, cut], minus_half[:, cut], ALU.pow)
                pool.drain()
                nc.gpsimd.tensor_tensor(shift1[:, cut], moments1[:, cut, 0], rstd1[:, cut], ALU.mult)
                pool.drain()
                nc.gpsimd.tensor_tensor(shift1[:, cut], zeros[:, cut], shift1[:, cut], ALU.subtract).then_inc(shift1_ready, 1)

            over_batches(pool, prepare, KT, main, finish, 2)
            pool.wait_ge(beyond_ready, 1)
            nc.gpsimd.partition_all_reduce(beyond_any[:], beyond[:], P, bass.bass_isa.ReduceOp.max).then_inc(beyond_reduced, 1)

        @block.scalar
        def _(act):
            def squash(b, t):
                act.wait_ge(scored, b * RT + t + 1)
                if t >= 2:
                    act.wait_ge(masked, b * RT + t - 1)
                elif later(b):
                    act.wait_ge(step_ready, b * (H * RT))
                width = N - t * P
                scores = score_banks(t)[:, 0:width]
                nc.scalar.activation(alpha[:, t % 2, 0:width], scores, ACT.Tanh, scale=0.5 / SCALE)
                nc.scalar.activation(scores, scores, ACT.Tanh, scale=0.5 * LEAK / SCALE).then_inc(squashed, 1)

            def prepare(b, part):
                if part == 0:
                    act.wait_ge(x_cols_in, b * 16 + 16)
                    nc.scalar.activation(cols_hi[:], x_cols[:], ACT.Copy).then_inc(cols_high, 1)
                    for c in range(KT):
                        last = nc.scalar.activation(gated_hi[:, c, :], x_cols[:, c, :], ACT.Copy, scale=gate[:, c:c + 1])
                    last.then_inc(gated_high, 1)
                else:
                    squash(b, 0)
                    squash(b, 1)

            def main(b, prepare_next, finish_last):
                def check_x():
                    nc.scalar.activation(unused, x_cols[:].rearrange("p c n -> p (c n)"), ACT.Square, accum_out=seen[:, RT:RT + 1]
                                         ).then_inc(x_checked, 1)
                    act.drain()

                def check_adj(t):
                    act.wait_ge(adj_in[t], b * 16 + 16)
                    nc.scalar.activation(unused[:, 0:N], adj_cols[:, t, :], ACT.Relu, bias=minus_one[:],
                                         accum_out=seen[:, t:t + 1]).then_inc(adj_checked, 1)
                    act.drain()

                for t in range(2, RT):
                    squash(b, t)
                    if t == 2:
                        finish_last(0)
                    elif t == 3:
                        check_x()
                    else:
                        check_adj(t - 4)
                for t in range(RT - 4, RT):
                    check_adj(t)
                prepare_next(0)

                def x1_part(t):
                    act.wait_ge(x1_turned, b * RT + t + 1)
                    nc.scalar.activation(x1_hi[:, t].rearrange("p c q -> p (c q)"), ps[:, t % 2, 0:D], ACT.Copy).then_inc(x1_high, 1)

                def rows_part(half):
                    act.wait_ge(rows_ready, b * 2 + half + 1)
                    nc.scalar.activation(src_rows[0:H, half * HN:(half + 1) * HN], ps[0:H, 2 + half, :], ACT.Copy, scale=1 / SCALE
                                         ).then_inc(rows_high, 1)

                def take_values(t):
                    if t == 0:
                        act.wait_ge(ones_set, b + 1)
                    act.wait_ge(values_ready, b * RT + t + 1)
                    product = ps[:, 4 + t % 2, :]
                    nc.scalar.activation(sd[:, t], product[:, D:DX].rearrange("p (s h) -> p s h", s=2), ACT.Copy, scale=1 / SCALE
                                         ).then_inc(sd_ready, 1)
                    nc.scalar.activation(values[:, t, :, 0:F], product[:, 0:D].rearrange("p (h f) -> p h f", h=H), ACT.Copy, scale=1 / SCALE
                                         ).then_inc(values_taken, 1)

                for t in range(RT + 2):
                    if t == 2:
                        for part in range(1, 1 + RT // 2):
                            finish_last(part)
                    if t < RT:
                        x1_part(t)
                    if t == RT + 1:
                        rows_part(1)
                    if t >= 2:
                        take_values(t - 2)
                    if t == RT // 2 + 1:
                        rows_part(0)
                    if t in (RT - 2, RT - 1):
                        finish_last(t - 1)
                finish_last(RT - 1)
                finish_last(RT)

                def copy_src(h):
                    act.wait_ge(src_spread, b * H + h + 1)
                    nc.scalar.activation(src_all[:, h, :], banks(SRC_BANKS[h], 2), ACT.Copy).then_inc(src_copied, 1)
                    act.drain()

                def lift(n):
                    if n in COMPARED:
                        return
                    h, t, k = n // RT, n % RT, LIFTED.index(n)
                    if k >= RING:
                        act.wait_ge(step_ready, b * (H * RT) + LIFTED[k - RING] + 1)
                    nc.scalar.activation(above[:, k % RING, :], src_all[:, h, :], ACT.Relu, bias=dst_steep[:, t, h:h + 1], scale=STEEP
                                         ).then_inc(above_ready, 1)

                def high_full(h):
                    if h == 0:
                        act.wait_ge(full_ready, b + 1)
                    else:
                        act.wait_ge(pool_full_ready, b * (H - 1) + h)
                    nc.scalar.activation(step_rhs[:, 0, :, h, 0:F1], prod_full[:, :, h, :], ACT.Copy).then_inc(full_high, 1)

                def high_leak(h):
                    act.wait_ge(leak_ready, b * H + h + 1)
                    nc.scalar.activation(edge_rhs[:, 0, :, h, :], leak_product(h), ACT.Copy).then_inc(leak_high, 1)

                copy_src(0)
                act.wait_ge(relative, b + 1)
                nc.scalar.activation(exp_full[:], dst_rel[:], ACT.Exp, bias=log_scale[:])
                nc.scalar.activation(exp_leak[:], dst_rel[:], ACT.Exp, bias=log_scale[:], scale=LEAK)
                nc.scalar.activation(exp_src[:], src_rel[:], ACT.Exp, scale=1 - LEAK).then_inc(exps_ready, 1)
                lift(0)
                high_full(0)
                high_leak(0)
                copy_src(1)
                for n in range(1, H * RT):
                    lift(n)
                    h, t = n // RT, n % RT
                    if n in (2, 6):
                        copy_src(2 + n // 4)
                    if t == 4 and h + 1 < H:
                        high_full(h + 1)
                    if t == 6 and h + 1 < H:
                        high_leak(h + 1)
                prepare_next(1)

            def finish(b, part):
                if part == 0:
                    act.wait_ge(negative_ready, b + 1)
                    nc.scalar.activation(grown, grown, ACT.Exp).then_inc(grown_ready, 1)
                else:
                    t = part - 1
                    act.wait_ge(shift1_ready, b * 2 + 1 + t // (RT // 2))
                    nc.scalar.activation(out_rows[:, t, :], out_rows[:, t, :], ACT.Identity,
                                         scale=rstd1[:, t:t + 1], bias=shift1[:, t:t + 1]).then_inc(out_ready, 1)

            act.wait_ge(w_whole, 1)
            nc.scalar.activation(W_hi[:], W_ext[:], ACT.Copy, scale=SCALE).then_inc(w_split, 1)
            over_batches(act, prepare, 2, main, finish, 1 + RT)

        @block.tensor
        def _(pe):
            pe.wait_ge(pool_consts, 1)
            pe.wait_ge(w_split, 3)
            for c in range(KT):
                last = nc.tensor.matmul(ps[:, 0, 0:D], ones[:], W_sq[:, c, 0:D], start=(c == 0), stop=(c == KT - 1))
            last.then_inc(norms_ready, 1)

            def score(b, t):
                if t == 0:
                    pe.wait_ge(cols_split, b * KT + KT)
                    pe.wait_ge(gated_split, b * KT + KT)
                    if later(b):
                        pe.wait_ge(sum_taken, b * RT)
                elif t == 1:
                    pe.wait_ge(bank_taken, b * (H * NG) - NG + 1 if later(b) else 1)
                elif t == 2:
                    pe.wait_ge(bank_taken, b * (H * NG) - NG + 2 if later(b) else 1)
                else:
                    pe.wait_ge(alpha_ready, b * RT + t - 1)
                own = slice(t * P, (t + 1) * P)
                for start in range(t * P, N, BANK):
                    cut = slice(start, min(start + BANK, N))
                    dst = score_banks(t)[:, cut.start - t * P:cut.stop - t * P]
                    terms = [(lhs, rhs, c) for lhs, rhs in ((gated_hi, cols_hi), (gated_hi, cols_lo), (gated_lo, cols_hi))
                             for c in range(KT)]
                    for n, (lhs, rhs, c) in enumerate(terms):
                        last = nc.tensor.matmul(dst, lhs[:, c, own], rhs[:, c, cut], start=(n == 0), stop=(n == len(terms) - 1))
                last.then_inc(scored, 1)

            def main(b, prepare_next, finish_last):
                def turn(t):
                    pe.wait_ge(alpha_ready, b * RT + t + 1)
                    if t == 0:
                        pe.wait_ge(bank_taken, b * (H * NG) + 1)
                    if t >= 1:
                        pe.wait_ge(masked, b * RT + t)
                    for j in range(RT - 1 - t):
                        last = nc.tensor.transpose(banks(4, 2)[:, j * P:(j + 1) * P], alpha[:, t % 2, (j + 1) * P:(j + 2) * P], ident[:])
                    last.then_inc(turned, 1)

                def add_up(t):
                    pe.wait_ge(masked, b * RT + t + 1)
                    if t == 0:
                        pe.wait_ge(x_rows_in, b * 16 + 16)
                    if t >= 2:
                        pe.wait_ge(sum_taken, b * RT + t - 1)
                    for j in range(RT):
                        last = nc.tensor.matmul(ps[:, 6 + t % 2, 0:D], weights[:, j, t * P:(t + 1) * P], x_rows[:, j, :],
                                                start=(j == 0), stop=(j == RT - 1))
                    last.then_inc(summed, 1)

                def turn_x1(t):
                    pe.wait_ge(x1_ready, b * RT + t + 1)
                    if t == 0:
                        pe.wait_ge(alpha_ready, b * RT + RT)
                    if t >= 2:
                        pe.wait_ge(x1_split, b * RT + t - 1)
                    for c in range(KT):
                        last = nc.tensor.transpose(ps[:, t % 2, c * P:(c + 1) * P], x1_rows[:, t, c * P:(c + 1) * P], ident[:])
                    last.then_inc(x1_turned, 1)

                def value(t):
                    pe.wait_ge(x1_split, b * RT + t + 1)
                    if t >= 2:
                        pe.wait_ge(values_taken, b * RT + t - 1)
                    terms = [(lhs, rhs, c) for lhs, rhs in ((x1_hi, W_hi), (x1_hi, W_lo), (x1_lo, W_hi)) for c in range(KT)]
                    for n, (cols, w, c) in enumerate(terms):
                        last = nc.tensor.matmul(ps[0:H, 2 + t // 4, t % 4 * P:(t % 4 + 1) * P], w[:, c, D:D + H], cols[:, t, c, :],
                                                start=(n == 0), stop=(n == len(terms) - 1))
                    if t % 4 == 3:
                        last.then_inc(rows_ready, 1)
                    for n, (cols, w, c) in enumerate(terms):
                        last = nc.tensor.matmul(ps[:, 4 + t % 2, 0:DX], cols[:, t, c, :], w[:, c, :],
                                                start=(n == 0), stop=(n == len(terms) - 1))
                    last.then_inc(values_ready, 1)

                for s in range(1, RT + 2):
                    if s + 1 < RT:
                        score(b, s + 1)
                    if s - 1 < RT - 1:
                        turn(s - 1)
                    if 0 <= s - 2:
                        add_up(s - 2)
                    if s >= RT:
                        for t in (2 * (s - RT), 2 * (s - RT) + 1):
                            turn_x1(t)
                            if t >= 2:
                                value(t - 2)
                for t in range(RT - 4, RT):
                    turn_x1(t)
                    value(t - 2)
                for t in range(RT - 2, RT):
                    value(t)
                def spread(h):
                    if h == 2:
                        pe.wait_ge(values_taken, b * RT + RT)
                    if h == 3:
                        pe.wait_ge(src_copied, b * H + 3)
                    for half in range(2):
                        last = nc.tensor.matmul(ps[:, SRC_BANKS[h] + half, :], head_pick[:, h, :], src_rows[:, half * HN:(half + 1) * HN],
                                                start=True, stop=True)
                    last.then_inc(src_spread, 1)

                pe.wait_ge(rows_split, b * 2 + 2)
                for h in range(3):
                    spread(h)
                prepare_next(0)
                for h in range(H):
                    if h < 2:
                        pe.wait_ge(src_copied, b * H + 2 + 2 * h)
                    pe.wait_ge(rhs_ready, b * H + h + 1)
                    if h >= 2:
                        pe.wait_ge(bank_taken, b * (H * NG) + (h - 1) * NG + 1)
                    for j in range(RT):
                        n = h * RT + j
                        pe.wait_ge(step_ready, b * (H * RT) + n + 1)
                        rested = n in RESTED
                        if rested:
                            pe.wait_ge(rest_ready, b * NR + RESTED.index(n) + 1)
                            without = rest[RESTED.index(n) % REST_RING]
                        for i in range(RT):
                            own, at = slice(i * P, (i + 1) * P), i % 3 * 2 * F1
                            bank = ps[:, h % 2 * 3 + i // 3, :]
                            width = F1 if rested else 2 * F1
                            for part in range(2):
                                nc.tensor.matmul(bank[:, at:at + width], step[:, n % RT, own], step_rhs[:, part, j, h, 0:width],
                                                 start=(i % 3 == 0 and j == 0 and part == 0), stop=False, skip_group_check=True)
                            for part in range(2):
                                lhs = without[:, own] if rested else edge[:, j, own]
                                last = nc.tensor.matmul(bank[:, at + F1:at + 2 * F1], lhs, edge_rhs[:, part, j, h, :],
                                                        start=False, stop=(j == RT - 1 and part == 1), skip_group_check=True)
                        last.then_inc(step_used, 1)
                        if h == 0 and j == 1:
                            spread(3)
                prepare_next(1)

            over_batches(pe, score, 2, main, nothing, 0)

        @block.vector
        def _(dve):
            def constants():
                dve.wait_ge(constants_in, 80)
                nc.vector.memset(ones[:], 1.0)
                nc.vector.memset(minus_half[:], -0.5)
                nc.vector.memset(zeros[:], 0.0)
                nc.vector.memset(log_scale[:], LOG_VALUE_SCALE)
                nc.vector.memset(minus_one[:], -1.0)
                nc.vector.memset(worst[:], -1.0)
                nc.vector.memset(seen[:], -1.0)
                nc.vector.memset(limit[:, 0:RT], 0.0)
                for n, most in enumerate((SQUARES_MOST, RANGE_MOST, SHIFT_MOST, 0.0, W_SQ_MOST, W_NORM_MOST, GATE_SQ_MOST)):
                    at = CHECK_AT[n]
                    nc.vector.memset(limit[:, at:CHECK_AT[n + 1]], most)
                nc.vector.tensor_scalar(gate[:], gate_in[:, :, 0], SCALE, None, ALU.mult).then_inc(consts_made, 1)
                for c in range(KT):
                    for s in range(2):
                        nc.vector.tensor_tensor(wa_prod[:, c, s, :], W_ext[:, c, 0:D], a_all[:, s, :], ALU.mult)
                dve.drain()
                for c in range(KT):
                    for s in range(2):
                        nc.vector.reduce_sum(W_ext[:, c, D + s * H:D + (s + 1) * H], wa_prod[:, c, s, :].rearrange("p (h f) -> p h f", h=H), AX_X)
                dve.drain()
                nc.vector.tensor_tensor(gate_sq[:], gate_in[:, :, 0], gate_in[:, :, 0], ALU.mult)
                nc.vector.tensor_tensor(W_sq, W_ext[:], W_ext[:], ALU.mult).then_inc(w_whole, 1)
                dve.drain()
                nc.vector.tensor_reduce(worst[:, CHECK_AT[4]:CHECK_AT[4] + 1], W_sq, AX_XY, ALU.max)
                nc.vector.tensor_reduce(worst[:, CHECK_AT[6]:CHECK_AT[6] + 1], gate_sq[:], AX_X, ALU.max)
                dve.wait_ge(w_split, 1)
                nc.vector.scalar_tensor_tensor(W_lo[:], W_ext[:], SCALE, W_hi[:], ALU.mult, ALU.subtract).then_inc(w_split, 2)
                dve.wait_ge(norms_ready, 1)
                nc.vector.reduce_max(worst[:, CHECK_AT[5]:CHECK_AT[5] + 1], ps[:, 0, 0:D], AX_X).then_inc(bank_taken, 1)
                dve.drain()

            def build_edge(b, t):
                dve.wait_ge(adj_in[t], b * 16 + 16)
                if later(b):
                    dve.wait_ge(step_used, b * (H * RT) - RT + t + 1)
                nc.vector.tensor_scalar(edge[:, t, :], adj_cols[:, t, :], 1.0, None, ALU.is_equal).then_inc(edge_built, 1)

            def leak(b, t):
                width = N - t * P
                dve.wait_ge(squashed, b * RT + t + 1)
                nc.vector.tensor_tensor(alpha[:, t % 2, 0:width], alpha[:, t % 2, 0:width], score_banks(t)[:, 0:width],
                                        ALU.max).then_inc(alpha_ready, 1)

            def mask_own(b, t):
                width = N - t * P
                dve.wait_ge(alpha_ready, b * RT + t + 1)
                last = nc.vector.scalar_tensor_tensor(weights[:, t, t * P:N], alpha[:, t % 2, 0:width], 1.0, edge[:, t, t * P:N],
                                                      ALU.add, ALU.mult)
                if t == RT - 1:
                    last.then_inc(masked, 1)

            def prepare(b, part):
                if part < KT:
                    dve.wait_ge(gated_high, b + 1)
                    nc.vector.scalar_tensor_tensor(gated_lo[:, part, :], x_cols[:, part, :], gate[:, part:part + 1], gated_hi[:, part, :],
                                                   ALU.mult, ALU.subtract).then_inc(gated_split, 1)
                elif part == KT:
                    for t in range(RT - 1):
                        build_edge(b, t)
                        if t == RT // 2:
                            leak(b, 0)
                            mask_own(b, 0)
                else:
                    build_edge(b, RT - 1)

            def main(b, prepare_next, finish_last):
                def mask_turned(t):
                    dve.wait_ge(turned, b * (RT - 1) + t + 1)
                    nc.vector.scalar_tensor_tensor(
                        weights[:, t + 1:RT, t * P:(t + 1) * P],
                        banks(4, 2)[:, 0:(RT - 1 - t) * P].rearrange("p (j q) -> p j q", q=P),
                        1.0, edge[:, t + 1:RT, t * P:(t + 1) * P], ALU.add, ALU.mult).then_inc(masked, 1)

                def take_sum(t):
                    if t == 0:
                        dve.wait_ge(biased, b + 1)
                    dve.wait_ge(summed, b * RT + t + 1)
                    nc.vector.scalar_tensor_tensor(x1_rows[:, t, :], ps[:, 6 + t % 2, 0:D], 0.5, x_bias[:, t, :],
                                                   ALU.mult, ALU.add).then_inc(sum_taken, 1)
                    dve.drain()
                    nc.vector.bn_stats(stats[:, t, :], x1_rows[:, t, :])
                    dve.drain()
                    nc.vector.bn_aggr(moments[:, t, :], stats[:, t, :])
                    dve.drain()
                    nc.vector.tensor_scalar(var[:, t:t + 1], moments[:, t, 1:2], LN_EPS, None, ALU.add).then_inc(var_ready, 1)

                def normalise(t):
                    dve.wait_ge(rstd_ready, b * RT + t + 1)
                    nc.vector.tensor_scalar(x1_rows[:, t, :], x1_rows[:, t, :], moments[:, t, 0:1], rstd[:, t:t + 1],
                                            ALU.subtract, ALU.mult).then_inc(x1_ready, 1)

                def split_x1(t):
                    dve.wait_ge(x1_high, b * RT + t + 1)
                    nc.vector.tensor_tensor(x1_lo[:, t].rearrange("p c q -> p (c q)"), ps[:, t % 2, 0:D],
                                            x1_hi[:, t].rearrange("p c q -> p (c q)"), ALU.subtract).then_inc(x1_split, 1)

                def split_rows(half):
                    dve.wait_ge(rows_high, b * 2 + half + 1)
                    cut = slice(half * HN, (half + 1) * HN)
                    nc.vector.scalar_tensor_tensor(src_rows[32:32 + H, cut], ps[0:H, 2 + half, :], 1 / SCALE, src_rows[0:H, cut],
                                                   ALU.mult, ALU.subtract).then_inc(rows_split, 1)

                dve.drain()
                for s in range(1, RT + 2):
                    if s < RT:
                        leak(b, s)
                    if s - 1 < RT - 1:
                        mask_turned(s - 1)
                    if s < RT:
                        mask_own(b, s)
                    if s == 1:
                        finish_last(0)
                    if s == 2:
                        finish_last(1)
                        finish_last(2)
                        nc.vector.memset(values[:, :, :, F:F1], 1.0).then_inc(ones_set, 1)
                    if s >= 3:
                        finish_last(s)
                    if 0 <= s - 3:
                        take_sum(s - 3)
                    if 0 <= s - 4:
                        normalise(s - 4)
                    if s == RT + 1:
                        split_x1(0)
                        split_x1(1)
                take_sum(RT - 1)
                normalise(RT - 2)
                split_x1(2)
                normalise(RT - 1)
                split_x1(3)
                finish_last(10)
                split_x1(4)
                split_x1(5)
                prepare_next(0)
                split_x1(6)
                split_rows(0)
                split_x1(7)
                prepare_next(1)
                split_rows(1)
                dve.wait_ge(sd_ready, b * RT + RT)
                nc.vector.tensor_scalar(dst_neg[:], sd[:, :, 1, :], -1.0, None, ALU.mult)
                nc.vector.tensor_scalar(dst_steep[:], sd[:, :, 1, :], STEEP, None, ALU.mult)
                nc.vector.reduce_max(peaks[:, 0:2, :], sd[:].rearrange("p t s h -> p s h t"), AX_X)
                dve.drain()
                nc.vector.reduce_max(peaks[:, 2, :], dst_neg[:].rearrange("p t h -> p h t"), AX_X).then_inc(peaks_ready, 1)

                def make_step(n):
                    if n >= RT:
                        dve.wait_ge(step_used, b * (H * RT) + n - RT + 1)
                    if n in COMPARED:
                        h, t = n // RT, n % RT
                        dve.wait_ge(src_copied, b * H + h + 1)
                        nc.vector.scalar_tensor_tensor(step[:, t, :], src_all[:, h, :], dst_neg[:, t, h:h + 1], edge[:, t, :],
                                                       ALU.is_gt, ALU.mult).then_inc(step_ready, 1)
                    else:
                        k = LIFTED.index(n)
                        dve.wait_ge(above_ready, b * NL + k + 1)
                        nc.vector.tensor_tensor(step[:, n % RT, :], above[:, k % RING, :], edge[:, n % RT, :], ALU.min
                                                ).then_inc(step_ready, 1)

                def weigh_full(h):
                    nc.vector.tensor_tensor(prod_full[:, :, h, :], values[:, :, h, :], exp_full[:, :, h:h + 1].to_broadcast([P, RT, F1]),
                                            ALU.mult).then_inc(full_ready, 1)

                def split_full(h):
                    dve.wait_ge(full_high, b * H + h + 1)
                    nc.vector.tensor_tensor(step_rhs[:, 1, :, h, 0:F1], prod_full[:, :, h, :], step_rhs[:, 0, :, h, 0:F1], ALU.subtract)

                def split_leak(h):
                    dve.wait_ge(leak_high, b * H + h + 1)
                    nc.vector.tensor_tensor(edge_rhs[:, 1, :, h, :], leak_product(h), edge_rhs[:, 0, :, h, :], ALU.subtract)
                    dve.drain()
                    negate_leak(h)

                def negate_leak(h):
                    nc.vector.tensor_scalar(step_rhs[:, :, :, h, F1:2 * F1].rearrange("p k t f -> p (k t) f"),
                                            edge_rhs[:, :, :, h, :].rearrange("p k t f -> p (k t) f"), -1.0, None, ALU.mult
                                            ).then_inc(rhs_ready, 1)

                def take_head(h):
                    dve.drain()
                    sums = [ps[:, h % 2 * 3 + g, 0:count * 2 * F1].rearrange("p (t k f) -> p t k f", t=count, k=2)
                            for g, (t0, count) in enumerate(GROUPS)]
                    for g, (t0, count) in enumerate(GROUPS):
                        dve.wait_ge(step_used, b * (H * RT) + h * RT + RT)
                        nc.vector.tensor_tensor(boosted[:, t0:t0 + count, :], sums[g][:, :, 0, :],
                                                exp_src[:, t0:t0 + count, h:h + 1].to_broadcast([P, count, F1]), ALU.mult)
                    dve.drain()
                    for g, (t0, count) in enumerate(GROUPS):
                        nc.vector.tensor_tensor(attended[:, t0:t0 + count, h, :], boosted[:, t0:t0 + count, :], sums[g][:, :, 1, :],
                                                ALU.add).then_inc(bank_taken, 1)

                def invert(h):
                    dve.drain()
                    nc.vector.tensor_scalar(inv_sum[:, :, h], attended[:, :, h, F], TINY, None, ALU.max)
                    dve.drain()
                    last = nc.vector.reciprocal(inv_sum[:, :, h], inv_sum[:, :, h])
                    if h == H - 1:
                        last.then_inc(inverted, 1)
                    else:
                        dve.drain()
                        nc.vector.tensor_tensor(attended[:, :, h, 0:F], attended[:, :, h, 0:F],
                                                inv_sum[:, :, h:h + 1].to_broadcast([P, RT, F]), ALU.mult)

                dve.wait_ge(tops_ready, b + 1)
                top = tops[:, 1:2, :].to_broadcast([P, RT, H])
                nc.vector.tensor_tensor(dst_rel[:], sd[:, :, 1, :], top, ALU.subtract)
                nc.vector.tensor_tensor(src_rel[:], sd[:, :, 0, :], top, ALU.add)
                dve.drain()
                nc.vector.tensor_scalar(src_rel[:], src_rel[:], SHIFT_MOST, None, ALU.min).then_inc(relative, 1)
                nc.vector.tensor_tensor(seen[:, CHECK_AT[1]:CHECK_AT[2]], tops[:, 2, :], tops[:, 1, :], ALU.add)
                nc.vector.tensor_tensor(seen[:, CHECK_AT[2]:CHECK_AT[3]], tops[:, 0, :], tops[:, 1, :], ALU.add)
                dve.drain()
                dve.wait_ge(exps_ready, b + 1)
                weigh_full(0)
                nc.vector.tensor_tensor(worst[:, 0:CHECK_AT[3]], worst[:, 0:CHECK_AT[3]], seen[:, 0:CHECK_AT[3]], ALU.max)
                make_step(0)
                split_full(0)
                split_leak(0)
                for n in range(1, H * RT):
                    make_step(n)
                    h, t = n // RT, n % RT
                    if h >= 1 and t == 2:
                        dve.wait_ge(pool_split, b * (2 * H - 2) + 2 * h)
                        negate_leak(h)
                    if h >= 1 and t == 4:
                        take_head(h - 1)
                        invert(h - 1)
                prepare_next(KT)
                take_head(H - 1)
                invert(H - 1)
                prepare_next(KT + 1)

            def finish(b, part):
                x1_heads = x1_rows[:].rearrange("p t (h f) -> p (t h) f", h=H)
                out_heads = out_rows.rearrange("p t (h f) -> p (t h) f", h=H)
                if part == 0:
                    nc.vector.tensor_reduce(least[:], attended[:, :, :, F], AX_XY, ALU.min)
                    dve.wait_ge(divided, b + 1)
                    nc.vector.tensor_scalar(grown, heads[:, :, 0:F], 0.0, None, ALU.min).then_inc(negative_ready, 1)
                    dve.drain()
                    nc.vector.tensor_scalar(seen[:, CHECK_AT[3]:CHECK_AT[4]], least[:], TINY, None, ALU.is_le)
                    dve.drain()
                    nc.vector.tensor_tensor(worst[:, CHECK_AT[3]:CHECK_AT[4]], worst[:, CHECK_AT[3]:CHECK_AT[4]],
                                            seen[:, CHECK_AT[3]:CHECK_AT[4]], ALU.max)
                elif part <= 2:
                    dve.drain()
                    dve.wait_ge(grown_ready, b + 1)
                    cut = slice((part - 1) * RT * H // 2, part * RT * H // 2)
                    nc.vector.scalar_tensor_tensor(out_heads[:, cut], grown[:, cut], -1.0, x1_heads[:, cut], ALU.add, ALU.add)
                    dve.drain()
                else:
                    t = part - 3
                    cut = slice(t * H, (t + 1) * H)
                    nc.vector.scalar_tensor_tensor(out_heads[:, cut], heads[:, cut, 0:F], 0.0, out_heads[:, cut], ALU.max, ALU.add)
                    dve.drain()
                    nc.vector.bn_stats(stats1[:, t, :], out_rows[:, t, :])
                    dve.drain()
                    nc.vector.bn_aggr(moments1[:, t, :], stats1[:, t, :])
                    dve.drain()
                    nc.vector.tensor_scalar(var1[:, t:t + 1], moments1[:, t, 1:2], LN_EPS, None, ALU.add).then_inc(var1_ready, 1)

            constants()
            over_batches(dve, prepare, KT + 2, main, finish, 11)
            dve.drain()
            nc.vector.tensor_tensor(limit[:], worst[:], limit[:], ALU.is_gt)
            dve.drain()
            nc.vector.reduce_max(beyond[:], limit[:], AX_X).then_inc(beyond_ready, 1)
            dve.wait_ge(beyond_reduced, 1)
            nc.vector.tensor_copy(flag_sb[:], beyond_any[0:1, :])


def general_path(nc, x, xT, adj, gates, bias, W, a_src, a_dst, out, flag_sb):
    B, N, D = x.shape
    H, F = a_src.shape
    KT, RT, TYPES = D // P, N // P, gates.shape[2]
    HN = N // 2

    with ExitStack() as ctx:
        def sb(name, shape, dt=F32):
            return ctx.enter_context(nc.sbuf_tensor("g_" + name, shape, dt))

        def ps(name, shape, dt=F32):
            return ctx.enter_context(nc.psum_tensor("g_" + name, shape, dt))

        def sem(name):
            return ctx.enter_context(nc.semaphore("g_" + name))

        h_rows = sb("h_rows", [P, RT, D])
        h_cols = sb("h_cols", [P, KT, N])
        adj_rows = sb("adj_rows", [P, N], I32)
        gate_cols = sb("gate_cols", [P, KT, TYPES])
        bias_all = sb("bias_all", [P, D])
        W_sb = sb("W_sb", [P, KT, D])
        a_all = sb("a_all", [P, 2, D])
        wa_prod = sb("wa_prod", [P, D])
        wa = sb("wa", [P, KT, 2, H])
        wa_wide = sb("wa_wide", [P, KT, H, P])
        ones = sb("ones", [P, P])
        ident = sb("ident", [P, P])
        gated = sb("gated", [P, KT, P])
        picked = sb("picked", [P, N])
        scores = sb("scores", [P, N])
        in_range = sb("in_range", [P, N])
        weights = sb("weights", [P, N])
        masked = sb("masked", [P, N])
        weights_T = sb("weights_T", [P, RT, P])
        row = sb("row", [P, D])
        stats = sb("stats", [P, 6])
        moments = sb("moments", [P, 2])
        var = sb("var", [P, 1])
        std = sb("std", [P, 1])
        x1_rows = sb("x1_rows", [P, RT, D])
        x1_cols = sb("x1_cols", [P, KT, N])
        values = sb("values", [P, RT, D])
        src = sb("src", [P, RT, H])
        dst_all = sb("dst_all", [P, H, N])
        mask = sb("mask", [P, N])
        penalty = sb("penalty", [P, N])
        row_max = sb("row_max", [P, 1])
        row_sum = sb("row_sum", [P, 1])
        attended = sb("attended", [P, D])
        negative = sb("negative", [P, D])
        grown = sb("grown", [P, D])

        score_ps = ps("score_ps", [P, N])
        turn_ps = ps("turn_ps", [P, N])
        row_ps = ps("row_ps", [P, 512])
        wide_ps = ps("wide_ps", [P, 512])

        flag_in = sem("flag_in")
        constants_in = sem("constants_in")
        batch_in = sem("batch_in")
        adj_in = sem("adj_in")
        adj_used = sem("adj_used")
        stored = sem("stored")
        ident_zero = sem("ident_zero")
        ident_ready = sem("ident_ready")
        folded = sem("folded")
        gated_ready = sem("gated_ready")
        scores_ready = sem("scores_ready")
        leaked = sem("leaked")
        squashed = sem("squashed")
        masked_ready = sem("masked_ready")
        turned = sem("turned")
        turned_copied = sem("turned_copied")
        summed = sem("summed")
        var_ready = sem("var_ready")
        std_ready = sem("std_ready")
        x1_ready = sem("x1_ready")
        x1_turned = sem("x1_turned")
        x1_whole = sem("x1_whole")
        values_ready = sem("values_ready")
        values_copied = sem("values_copied")
        dst_ready = sem("dst_ready")
        dst_copied = sem("dst_copied")
        exp_in = sem("exp_in")
        exp_out = sem("exp_out")
        exp_turned = sem("exp_turned")
        exp_copied = sem("exp_copied")
        head_summed = sem("head_summed")
        negative_ready = sem("negative_ready")
        grown_ready = sem("grown_ready")
        out_ready = sem("out_ready")
        batch_done = sem("batch_done")

        def sync_program(sp):
            sp.dma_start(gate_cols[:], gates).then_inc(constants_in, 16)
            sp.dma_start(bias_all[:], bias.partition_broadcast(P)).then_inc(constants_in, 16)
            sp.dma_start(W_sb[:], W.rearrange("(c p) n -> p c n", p=P)).then_inc(constants_in, 16)
            for s, a in enumerate((a_src, a_dst)):
                sp.dma_start(a_all[:, s, :], a.rearrange("h f -> (h f)").partition_broadcast(P)).then_inc(constants_in, 16)
            with sp.Fori(0, B) as b:
                sp.wait_ge(batch_done, b + 1)
                sp.dma_start(h_rows[:], x[bass.ds(b, 1)].rearrange("a (t p) d -> p (a t) d", p=P)).then_inc(batch_in, 16)
                sp.dma_start(h_cols[:], xT[bass.ds(b, 1)].rearrange("a (c p) n -> p (a c) n", p=P)).then_inc(batch_in, 16)
                with sp.Fori(0, RT) as t:
                    sp.wait_ge(adj_used, b * (2 * RT) + t + 1)
                    sp.dma_start(adj_rows[:], adj[bass.ds(b, 1), bass.ds(t * P, P)].rearrange("a p n -> p (a n)")
                                 ).then_inc(adj_in, 16)
                with sp.Fori(0, RT) as t:
                    sp.wait_ge(adj_used, b * (2 * RT) + t + RT + 1)
                    sp.dma_start(adj_rows[:], adj[bass.ds(b, 1), bass.ds(t * P, P)].rearrange("a p n -> p (a n)")
                                 ).then_inc(adj_in, 16)
                    sp.wait_ge(out_ready, b * RT + t + 1)
                    sp.dma_start(out[bass.ds(b, 1), bass.ds(t * P, P)].rearrange("a p n -> p (a n)"), row[:]
                                 ).then_inc(stored, 16)
            sp.wait_ge(stored, B * RT * 16)

        def gpsimd_program(pool):
            nc.gpsimd.memset(ident[:], 0.0).then_inc(ident_zero, 1)
            pool.wait_ge(ident_zero, 1)
            nc.gpsimd.affine_select(out=ident[:], in_=ident[:], compare_op=ALU.not_equal, fill=1.0,
                                    base=0, pattern=[[-1, P]], channel_multiplier=1).then_inc(ident_ready, 1)

        def scalar_program(act):
            with act.Fori(0, B) as b:
                with act.Fori(0, RT) as t:
                    act.wait_ge(leaked, b * RT + t + 1)
                    nc.scalar.activation(weights[:], scores[:], ACT.Sigmoid).then_inc(squashed, 1)
                    act.wait_ge(var_ready, b * (2 * RT) + t + 1)
                    nc.scalar.activation(std[:], var[:], ACT.Sqrt).then_inc(std_ready, 1)
                with act.Fori(0, RT) as t:
                    for h in range(H):
                        act.wait_ge(exp_in, (b * RT + t) * H + h + 1)
                        nc.scalar.activation(weights[:], scores[:], ACT.Exp, accum_out=row_sum[:]).then_inc(exp_out, 1)
                    act.wait_ge(negative_ready, b * RT + t + 1)
                    nc.scalar.activation(grown[:], negative[:], ACT.Exp).then_inc(grown_ready, 1)
                    act.wait_ge(var_ready, b * (2 * RT) + t + RT + 1)
                    nc.scalar.activation(std[:], var[:], ACT.Sqrt).then_inc(std_ready, 1)

        def tensor_program(pe):
            pe.wait_ge(ident_ready, 1)
            pe.wait_ge(folded, 1)
            with pe.Fori(0, B) as b:
                with pe.Fori(0, RT) as t:
                    n = b * RT + t
                    pe.wait_ge(batch_in, b * 32 + 32)
                    for k in range(TYPES):
                        pe.wait_ge(gated_ready, n * TYPES + k + 1)
                        for half in range(2):
                            cut = slice(half * HN, (half + 1) * HN)
                            for c in range(KT):
                                last = nc.tensor.matmul(score_ps[:, cut], gated[:, c, :], h_cols[:, c, cut],
                                                        start=(c == 0), stop=(c == KT - 1))
                        last.then_inc(scores_ready, 1)
                    pe.wait_ge(masked_ready, n + 1)
                    for j in range(RT):
                        last = nc.tensor.transpose(turn_ps[:, j * P:(j + 1) * P], masked[:, j * P:(j + 1) * P], ident[:])
                    last.then_inc(turned, 1)
                    pe.wait_ge(turned_copied, n + 1)
                    for j in range(RT):
                        last = nc.tensor.matmul(row_ps[:, 0:D], weights_T[:, j, :], h_rows[:, j, :],
                                                start=(j == 0), stop=(j == RT - 1))
                    last.then_inc(summed, 1)
                    pe.wait_ge(x1_ready, n + 1)
                    for c in range(KT):
                        last = nc.tensor.transpose(wide_ps[:, c * P:(c + 1) * P], row[:, c * P:(c + 1) * P], ident[:])
                    last.then_inc(x1_turned, 1)
                pe.wait_ge(x1_whole, b + 1)
                for t in range(RT):
                    if t >= 1:
                        pe.wait_ge(values_copied, b * RT + t)
                    for c in range(KT):
                        nc.tensor.matmul(row_ps[:, 0:D], x1_cols[:, c, t * P:(t + 1) * P], W_sb[:, c, :],
                                         start=(c == 0), stop=(c == KT - 1))
                    for c in range(KT):
                        last = nc.tensor.matmul(wide_ps[:, 0:H], x1_cols[:, c, t * P:(t + 1) * P], wa[:, c, 0, :],
                                                start=(c == 0), stop=(c == KT - 1))
                    last.then_inc(values_ready, 1)
                pe.wait_ge(values_copied, b * RT + RT)
                for n in range(2 * H):
                    cut = slice(n % 2 * HN, (n % 2 + 1) * HN)
                    if n >= 1:
                        pe.wait_ge(dst_copied, b * (2 * H) + n)
                    for c in range(KT):
                        last = nc.tensor.matmul(wide_ps[:, 0:HN], wa_wide[:, c, n // 2, :], x1_cols[:, c, cut],
                                                start=(c == 0), stop=(c == KT - 1))
                    last.then_inc(dst_ready, 1)
                with pe.Fori(0, RT) as t:
                    n = b * RT + t
                    for h in range(H):
                        pe.wait_ge(exp_out, n * H + h + 1)
                        for j in range(RT):
                            last = nc.tensor.transpose(turn_ps[:, j * P:(j + 1) * P], weights[:, j * P:(j + 1) * P], ident[:])
                        last.then_inc(exp_turned, 1)
                        pe.wait_ge(exp_copied, n * H + h + 1)
                        for j in range(RT):
                            last = nc.tensor.matmul(row_ps[:, 0:F], weights_T[:, j, :], values[:, j, h * F:(h + 1) * F],
                                                    start=(j == 0), stop=(j == RT - 1))
                        last.then_inc(head_summed, 1)

        def vector_program(dve):
            def std_of_row(nth):
                nc.vector.bn_stats(stats[:], row[:])
                dve.drain()
                nc.vector.bn_aggr(moments[:], stats[:])
                dve.drain()
                nc.vector.tensor_scalar_add(var[:], moments[:, 1:2], LN_EPS).then_inc(var_ready, 1)
                dve.wait_ge(std_ready, nth)
                nc.vector.reciprocal(var[:], std[:])
                dve.drain()

            nc.vector.memset(stats[:], 0.0).then_inc(batch_done, 1)
            nc.vector.memset(row_max[:], 0.0).then_inc(adj_used, 1)
            dve.wait_ge(constants_in, 80)
            nc.vector.memset(ones[:], 1.0)
            for c in range(KT):
                for s in range(2):
                    dve.drain()
                    nc.vector.tensor_tensor(wa_prod[:], W_sb[:, c, :], a_all[:, s, :], ALU.mult)
                    dve.drain()
                    nc.vector.reduce_sum(wa[:, c, s, :], wa_prod[:].rearrange("p (h f) -> p h f", h=H), AX_X)
            dve.drain()
            for c in range(KT):
                for h in range(H):
                    last = nc.vector.tensor_scalar(wa_wide[:, c, h, :], ones[:], wa[:, c, 1, h:h + 1], None, ALU.mult)
            last.then_inc(folded, 1)
            dve.drain()

            with dve.Fori(0, B) as b:
                with dve.Fori(0, RT) as t:
                    n = b * RT + t
                    dve.wait_ge(batch_in, b * 32 + 32)
                    dve.wait_ge(adj_in, (b * (2 * RT) + t) * 16 + 16)
                    for k in range(TYPES):
                        for c in range(KT):
                            last = nc.vector.tensor_scalar(gated[:, c, :], h_cols[:, c, bass.ds(t * P, P)],
                                                           gate_cols[:, c, k:k + 1], None, ALU.mult)
                        last.then_inc(gated_ready, 1)
                        dve.wait_ge(scores_ready, n * TYPES + k + 1)
                        dst = scores if k else picked
                        nc.vector.scalar_tensor_tensor(dst[:], adj_rows[:], float(k + 1), score_ps[:],
                                                       ALU.is_equal, ALU.mult)
                        dve.drain()
                        if k:
                            nc.vector.tensor_tensor(picked[:], picked[:], scores[:], ALU.add)
                            dve.drain()
                    nc.vector.scalar_tensor_tensor(scores[:], picked[:], LEAK, picked[:], ALU.mult, ALU.max).then_inc(leaked, 1)
                    nc.vector.tensor_scalar(in_range[:], adj_rows[:], 1.0, None, ALU.is_ge)
                    dve.drain()
                    nc.vector.scalar_tensor_tensor(penalty[:], adj_rows[:], float(TYPES), in_range[:],
                                                   ALU.is_le, ALU.mult).then_inc(adj_used, 1)
                    dve.drain()
                    dve.wait_ge(squashed, n + 1)
                    nc.vector.tensor_tensor(masked[:], weights[:], penalty[:], ALU.mult).then_inc(masked_ready, 1)
                    dve.wait_ge(turned, n + 1)
                    nc.vector.tensor_copy(weights_T[:].rearrange("p t q -> p (t q)"), turn_ps[:]).then_inc(turned_copied, 1)
                    dve.wait_ge(summed, n + 1)
                    nc.vector.tensor_tensor(row[:], row_ps[:, 0:D], bias_all[:], ALU.add)
                    dve.drain()
                    nc.vector.tensor_tensor(row[:], row[:], h_rows[:, bass.ds(t, 1), :].rearrange("p a d -> p (a d)"), ALU.add)
                    dve.drain()
                    std_of_row(b * (2 * RT) + t + 1)
                    nc.vector.tensor_scalar(row[:], row[:], moments[:, 0:1], var[:], ALU.subtract, ALU.mult).then_inc(x1_ready, 1)
                    dve.drain()
                    nc.vector.tensor_copy(x1_rows[:, bass.ds(t, 1), :].rearrange("p a d -> p (a d)"), row[:])
                    dve.wait_ge(x1_turned, n + 1)
                    nc.vector.tensor_copy(x1_cols[:, :, bass.ds(t * P, P)], wide_ps[:, 0:D].rearrange("p (c q) -> p c q", c=KT))
                    dve.drain()
                nc.vector.memset(stats[:], 0.0).then_inc(x1_whole, 1)
                for t in range(RT):
                    dve.wait_ge(values_ready, b * RT + t + 1)
                    nc.vector.tensor_copy(src[:, t, :], wide_ps[:, 0:H])
                    dve.drain()
                    nc.vector.tensor_copy(values[:, t, :], row_ps[:, 0:D]).then_inc(values_copied, 1)
                for m in range(2 * H):
                    dve.wait_ge(dst_ready, b * (2 * H) + m + 1)
                    nc.vector.tensor_copy(dst_all[:, m // 2, m % 2 * HN:(m % 2 + 1) * HN], wide_ps[:, 0:HN]).then_inc(dst_copied, 1)
                dve.drain()
                with dve.Fori(0, RT) as t:
                    n = b * RT + t
                    dve.wait_ge(adj_in, (b * (2 * RT) + t) * 16 + RT * 16 + 16)
                    nc.vector.tensor_scalar(mask[:], adj_rows[:], 0.0, None, ALU.is_gt).then_inc(adj_used, 1)
                    dve.drain()
                    nc.vector.tensor_scalar(penalty[:], mask[:], -NEG_INF, NEG_INF, ALU.mult, ALU.add)
                    dve.drain()
                    for h in range(H):
                        nc.vector.tensor_scalar(picked[:], dst_all[:, h, :], src[:, bass.ds(t, 1), h:h + 1].rearrange("p a h -> p (a h)"),
                                                None, ALU.add)
                        dve.drain()
                        nc.vector.scalar_tensor_tensor(scores[:], picked[:], LEAK, picked[:], ALU.mult, ALU.max)
                        dve.drain()
                        nc.vector.tensor_tensor(picked[:], scores[:], mask[:], ALU.mult)
                        dve.drain()
                        nc.vector.tensor_tensor(scores[:], picked[:], penalty[:], ALU.add)
                        dve.drain()
                        nc.vector.reduce_max(row_max[:], scores[:], AX_X)
                        dve.drain()
                        nc.vector.tensor_scalar(scores[:], scores[:], row_max[:], None, ALU.subtract).then_inc(exp_in, 1)
                        dve.wait_ge(exp_turned, n * H + h + 1)
                        nc.vector.tensor_copy(weights_T[:].rearrange("p t q -> p (t q)"), turn_ps[:]).then_inc(exp_copied, 1)
                        nc.vector.reciprocal(row_max[:], row_sum[:])
                        dve.drain()
                        dve.wait_ge(head_summed, n * H + h + 1)
                        nc.vector.tensor_scalar(attended[:, h * F:(h + 1) * F], row_ps[:, 0:F], row_max[:], None, ALU.mult)
                        dve.drain()
                    nc.vector.tensor_scalar(negative[:], attended[:], 0.0, None, ALU.min).then_inc(negative_ready, 1)
                    dve.wait_ge(grown_ready, n + 1)
                    nc.vector.tensor_scalar(grown[:], grown[:], 1.0, None, ALU.subtract)
                    dve.drain()
                    nc.vector.scalar_tensor_tensor(attended[:], attended[:], 0.0, grown[:], ALU.max, ALU.add)
                    dve.drain()
                    nc.vector.tensor_tensor(row[:], attended[:], x1_rows[:, bass.ds(t, 1), :].rearrange("p a d -> p (a d)"), ALU.add)
                    dve.drain()
                    std_of_row(b * (2 * RT) + t + RT + 1)
                    nc.vector.tensor_scalar(row[:], row[:], moments[:, 0:1], var[:], ALU.subtract, ALU.mult).then_inc(out_ready, 1)
                    dve.drain()
                    dve.wait_ge(stored, n * 16 + 16)
                nc.vector.memset(stats[:], 0.0).then_inc(batch_done, 1)
                dve.drain()

        block = ctx.enter_context(nc.Block())

        def when_flagged(eng, program):
            raw = eng.value_load(flag_sb[0:1, 0:1])
            with eng.If(raw > 0):
                program(eng)

        @block.sync
        def _(sp):
            when_flagged(sp, sync_program)

        @block.gpsimd
        def _(pool):
            when_flagged(pool, gpsimd_program)

        @block.scalar
        def _(act):
            when_flagged(act, scalar_program)

        @block.tensor
        def _(pe):
            when_flagged(pe, tensor_program)

        @block.vector
        def _(dve):
            when_flagged(dve, vector_program)


def build(nc, x, xT, adj, adjT, gates, bias, W, a_src, a_dst, out):
    with nc.sbuf_tensor("flag_sb", [1, 1], I32) as flag_sb:
        fast_path(nc, x, xT, adjT, gates, bias, W, a_src, a_dst, out, flag_sb)
        general_path(nc, x, xT, adj, gates, bias, W, a_src, a_dst, out, flag_sb)


def kernel(x, adj, L0_gnn_a0, L0_gnn_a1, L0_gnn_a2, L0_gnn_a3, L0_gnn_bias, L1_gnn_W, L1_gnn_a_src, L1_gnn_a_dst):
    import numpy as np
    import concourse.bacc as bacc
    from concourse.bass_utils import run_bass_kernel_spmd

    x, adj = np.asarray(x), np.asarray(adj)
    arrays = {
        "x": x,
        "xT": np.ascontiguousarray(x.transpose(0, 2, 1)),
        "adj": adj,
        "adjT": np.ascontiguousarray(adj.transpose(0, 2, 1)),
        "gates": np.ascontiguousarray(np.stack([np.asarray(a).reshape(-1, P).T for a in
                                                (L0_gnn_a0, L0_gnn_a1, L0_gnn_a2, L0_gnn_a3)], axis=2)),
        "bias": np.asarray(L0_gnn_bias),
        "W": np.asarray(L1_gnn_W),
        "a_src": np.asarray(L1_gnn_a_src),
        "a_dst": np.asarray(L1_gnn_a_dst),
    }
    nc = bacc.Bacc("TRN2", target_bir_lowering=False, num_devices=1)
    args = {n: nc.dram_tensor("in_" + n, a.shape, mybir.dt.from_np(a.dtype), kind="ExternalInput").ap()
            for n, a in arrays.items()}
    out = nc.dram_tensor("out", x.shape, F32, kind="ExternalOutput").ap()
    build(nc, **args, out=out)
    r = run_bass_kernel_spmd(nc, [{"in_" + n: a for n, a in arrays.items()}], core_ids=[0])
    return r.results[0]["out"]
```
